# Optimizing a Trainium2 kernel written in Bass

```python
import numpy as np
import jax
import jax.numpy as jnp

def _softmax(x, axis=-1):
    return jax.nn.softmax(x, axis=axis)

def _gelu(x):
    return jax.nn.gelu(x, approximate=True)

def _silu(x):
    return jax.nn.silu(x)

def _sigmoid(x):
    return jax.nn.sigmoid(x)

def _layernorm(x, axis=-1, eps=1e-05):
    m = jnp.mean(x, axis=axis, keepdims=True)
    v = jnp.var(x, axis=axis, keepdims=True)
    return (x - m) / jnp.sqrt(v + eps)

def _scatter_add(tgt, idx, src, axis=0):
    return tgt.at[idx].add(src)

def _segment_sum(src, seg, n):
    return jax.ops.segment_sum(src, seg, n)
kernel_name = 'mk_cond_resid_d4_seqx_r2_9fddeb'

def setup_inputs(seed: int=0):
    np.random.seed(seed)
    _w = jnp.asarray

    def _rec_inputs():
        import jax
        import jax.numpy as jnp
        _rk = jax.random.key(seed)
        x = -0.000125 + 0.9999 * jax.random.normal(jax.random.fold_in(_rk, 1), (4, 1024, 512), jnp.float32)
        _lenS = 1024 - jax.random.randint(jax.random.fold_in(_rk, 7), (4,), 0, max(1, 1024 // 4) + 1, jnp.int32)
        _lenS2 = 1024 - jax.random.randint(jax.random.fold_in(_rk, 8), (4,), 0, max(1, 1024 // 4) + 1, jnp.int32)
        cond_1024 = jax.random.uniform(jax.random.fold_in(_rk, 11), (4, 512), jnp.float32, 0.0, 0.999927)
        return (x, cond_1024)
    x, cond_1024 = _rec_inputs()

    def _L0_cond_setup():
        import jax, jax.numpy as jnp
        import numpy as np
        TEMPERATURE = 2.0
        key = jax.random.key(seed)
        k1, k2 = jax.random.split(key)
        B, N, D = (16, 1024, 512)
        x = jax.random.normal(k1, (B, N, D), dtype=jnp.float32)
        random_values = jax.random.uniform(k2, (B, D), dtype=jnp.float32)
        return {'x': x, 'random_values': random_values}
    _L0_cond_all = _L0_cond_setup()
    _L0_cond_in = {k: v for k, v in _L0_cond_all.items() if k in ()}
    del _L0_cond_all

    def _L1_cond_setup():
        import jax, jax.numpy as jnp
        import numpy as np
        N, T, D, H = (64, 256, 512, 512)

        def lstm_scan(x, h0, Wx, Wh, b):
            xW = jnp.einsum('ntd,dg->ntg', x, Wx) + b
            Hdim = h0.shape[1]
            c0 = jnp.zeros_like(h0)

            def step(carry, xw_t):
                prev_h, prev_c = carry
                a = xw_t + prev_h @ Wh
                i = jax.nn.sigmoid(a[:, :Hdim])
                f = jax.nn.sigmoid(a[:, Hdim:2 * Hdim])
                o = jax.nn.sigmoid(a[:, 2 * Hdim:3 * Hdim])
                g = jnp.tanh(a[:, 3 * Hdim:])
                next_c = f * prev_c + i * g
                next_h = o * jnp.tanh(next_c)
                return ((next_h, next_c), next_h)
            _, hs = jax.lax.scan(step, (h0, c0), jnp.swapaxes(xW, 0, 1))
            return jnp.swapaxes(hs, 0, 1)
        key = jax.random.key(seed)
        k1, k2, k3, k4 = jax.random.split(key, 4)
        x = jax.random.normal(k1, (N, T, D), dtype=jnp.float32)
        h0 = jax.random.normal(k2, (N, H), dtype=jnp.float32)
        Wx = jax.random.normal(k3, (D, 4 * H), dtype=jnp.float32) / np.sqrt(D)
        Wh = jax.random.normal(k4, (H, 4 * H), dtype=jnp.float32) / np.sqrt(H)
        b = jnp.zeros((4 * H,), dtype=jnp.float32)
        return {'x': x, 'h0': h0, 'Wx': Wx, 'Wh': Wh, 'b': b}
    _L1_cond_all = _L1_cond_setup()
    _L1_cond_in = {k: v for k, v in _L1_cond_all.items() if k in ('Wx', 'Wh', 'b')}
    del _L1_cond_all

    def _L2_cond_setup():
        import jax, jax.numpy as jnp
        import numpy as np
        EPS = 1e-08
        key = jax.random.key(seed)
        ks = jax.random.split(key, 8)
        B, S, D, H = (8, 1024, 512, 512)
        scale = 1.0 / np.sqrt(D)
        return {'input_seq': jax.random.normal(ks[0], (B, S, D), dtype=jnp.float32), 'initial_hidden': jax.random.normal(ks[1], (B, H), dtype=jnp.float32), 'W_f': jax.random.normal(ks[2], (H, D), dtype=jnp.float32) * scale, 'b_f': jnp.zeros((H,), dtype=jnp.float32), 'W_i': jax.random.normal(ks[3], (H, D), dtype=jnp.float32) * scale, 'b_i': jnp.zeros((H,), dtype=jnp.float32), 'W_h': jax.random.normal(ks[4], (H, D), dtype=jnp.float32) * scale, 'b_h': jnp.zeros((H,), dtype=jnp.float32)}
    _L2_cond_all = _L2_cond_setup()
    _L2_cond_in = {k: v for k, v in _L2_cond_all.items() if k in ('W_f', 'b_f', 'W_i', 'b_i', 'W_h', 'b_h')}
    del _L2_cond_all

    def _L3_cond_setup():
        import jax, jax.numpy as jnp
        import numpy as np
        N, T, D, H = (64, 256, 512, 512)
        key = jax.random.key(seed)
        k1, k2, k3, k4 = jax.random.split(key, 4)
        x = jax.random.normal(k1, (N, T, D), dtype=jnp.float32)
        h0 = jax.random.normal(k2, (N, H), dtype=jnp.float32)
        Wx = jax.random.normal(k3, (D, 4 * H), dtype=jnp.float32) / np.sqrt(D)
        Wh = jax.random.normal(k4, (H, 4 * H), dtype=jnp.float32) / np.sqrt(H)
        b = jnp.zeros((4 * H,), dtype=jnp.float32)
        return {'x': x, 'h0': h0, 'Wx': Wx, 'Wh': Wh, 'b': b}
    _L3_cond_all = _L3_cond_setup()
    _L3_cond_in = {k: v for k, v in _L3_cond_all.items() if k in ('Wx', 'Wh', 'b')}
    del _L3_cond_all
    return {'x': x, 'cond_1024': cond_1024, 'L1_cond_Wx': _L1_cond_in['Wx'], 'L1_cond_Wh': _L1_cond_in['Wh'], 'L1_cond_b': _L1_cond_in['b'], 'L2_cond_W_f': _L2_cond_in['W_f'], 'L2_cond_b_f': _L2_cond_in['b_f'], 'L2_cond_W_i': _L2_cond_in['W_i'], 'L2_cond_b_i': _L2_cond_in['b_i'], 'L2_cond_W_h': _L2_cond_in['W_h'], 'L2_cond_b_h': _L2_cond_in['b_h'], 'L3_cond_Wx': _L3_cond_in['Wx'], 'L3_cond_Wh': _L3_cond_in['Wh'], 'L3_cond_b': _L3_cond_in['b']}

def reference(x, cond_1024, L1_cond_Wx, L1_cond_Wh, L1_cond_b, L2_cond_W_f, L2_cond_b_f, L2_cond_W_i, L2_cond_b_i, L2_cond_W_h, L2_cond_b_h, L3_cond_Wx, L3_cond_Wh, L3_cond_b):
    import jax
    import jax.numpy as jnp

    def _L0_cond_ref(x, random_values):
        import jax, jax.numpy as jnp
        import numpy as np
        TEMPERATURE = 2.0
        ax = jnp.abs(x)
        p = ax / jnp.sum(ax, axis=1, keepdims=True)
        pi = jnp.exp(p * TEMPERATURE)
        thresholds = pi / jnp.sum(pi, axis=1, keepdims=True)
        cum = jnp.cumsum(thresholds, axis=1) + 0.001
        rv = random_values[:, None, :]
        chosen_idx = jnp.sum(cum <= rv, axis=1, keepdims=True)
        gathered = jnp.take_along_axis(ax, chosen_idx, axis=1)
        mask = ax >= gathered
        return x * mask

    def _L1_cond_ref(x, h0, Wx, Wh, b):
        import jax, jax.numpy as jnp
        import numpy as np
        N, T, D, H = (64, 256, 512, 512)

        def lstm_scan(x, h0, Wx, Wh, b):
            xW = jnp.einsum('ntd,dg->ntg', x, Wx) + b
            Hdim = h0.shape[1]
            c0 = jnp.zeros_like(h0)

            def step(carry, xw_t):
                prev_h, prev_c = carry
                a = xw_t + prev_h @ Wh
                i = jax.nn.sigmoid(a[:, :Hdim])
                f = jax.nn.sigmoid(a[:, Hdim:2 * Hdim])
                o = jax.nn.sigmoid(a[:, 2 * Hdim:3 * Hdim])
                g = jnp.tanh(a[:, 3 * Hdim:])
                next_c = f * prev_c + i * g
                next_h = o * jnp.tanh(next_c)
                return ((next_h, next_c), next_h)
            _, hs = jax.lax.scan(step, (h0, c0), jnp.swapaxes(xW, 0, 1))
            return jnp.swapaxes(hs, 0, 1)
        return lstm_scan(x, h0, Wx, Wh, b)

    def _L2_cond_ref(input_seq, initial_hidden, W_f, b_f, W_i, b_i, W_h, b_h):
        import jax, jax.numpy as jnp
        import numpy as np
        EPS = 1e-08
        forget_gate = jax.nn.sigmoid(jnp.einsum('bsd,hd->bsh', input_seq, W_f) + b_f)
        input_gate = jax.nn.sigmoid(jnp.einsum('bsd,hd->bsh', input_seq, W_i) + b_i)
        gate_sum = forget_gate + input_gate + EPS
        forget_norm = forget_gate / gate_sum
        input_norm = input_gate / gate_sum
        candidate = jnp.einsum('bsd,hd->bsh', input_seq, W_h) + b_h
        new_info = input_norm * candidate
        log_ret = jnp.log(forget_norm + EPS)
        log_cumprod = jnp.cumsum(log_ret, axis=1)
        B, _, H = log_cumprod.shape
        padded = jnp.concatenate([jnp.zeros((B, 1, H), dtype=log_cumprod.dtype), log_cumprod], axis=1)
        scaling = jnp.exp(log_cumprod[:, -1:, :] - padded[:, :-1, :])
        hidden = jnp.cumsum(scaling * new_info, axis=1)
        hidden = hidden + jnp.exp(log_cumprod) * initial_hidden[:, None, :]
        return hidden

    def _L3_cond_ref(x, h0, Wx, Wh, b):
        import jax, jax.numpy as jnp
        import numpy as np
        N, T, D, H = (64, 256, 512, 512)
        Hdim = h0.shape[1]
        xW = jnp.einsum('ntd,dg->ntg', x, Wx) + b
        c0 = jnp.zeros_like(h0)

        def step(carry, xw_t):
            prev_h, prev_c = carry
            A = xw_t + prev_h @ Wh
            i = jax.nn.sigmoid(A[:, 0:Hdim])
            f = jax.nn.sigmoid(A[:, Hdim:2 * Hdim])
            o = jax.nn.sigmoid(A[:, 2 * Hdim:3 * Hdim])
            g = jnp.tanh(A[:, 3 * Hdim:4 * Hdim])
            next_c = f * prev_c + i * g
            next_h = o * jnp.tanh(next_c)
            return ((next_h, next_c), next_h)
        _, hs = jax.lax.scan(step, (h0, c0), jnp.swapaxes(xW, 0, 1))
        return jnp.swapaxes(hs, 0, 1)
    x = x + _L0_cond_ref(x, cond_1024)
    x = x + _L1_cond_ref(x, cond_1024, L1_cond_Wx, L1_cond_Wh, L1_cond_b)
    x = x + _L2_cond_ref(x, cond_1024, L2_cond_W_f, L2_cond_b_f, L2_cond_W_i, L2_cond_b_i, L2_cond_W_h, L2_cond_b_h)
    x = x + _L3_cond_ref(x, cond_1024, L3_cond_Wx, L3_cond_Wh, L3_cond_b)
    return x

_drawn_inputs = setup_inputs


def setup_inputs(seed=0):
    import zlib

    import numpy as np

    out = dict(_drawn_inputs(seed))
    spreads = {'L1_cond_b': (0.0, 0.529),
     'L2_cond_b_f': (0.0, 0.8),
     'L2_cond_b_i': (0.0, 0.8),
     'L2_cond_b_h': (0.0, 0.8),
     'L3_cond_b': (0.0, 0.557)}
    factors = {'L2_cond_W_f': 8.0, 'L2_cond_W_i': 8.0, 'L2_cond_W_h': 6.547}
    for name, (base, spread) in spreads.items():
        noise = np.random.default_rng([zlib.crc32(name.encode()), seed]).standard_normal(out[name].shape)
        drawn = base * np.exp(spread * noise) if base else spread * noise
        out[name] = jnp.asarray(drawn.astype(out[name].dtype))
    for name, factor in factors.items():
        out[name] = (out[name] * factor).astype(out[name].dtype)
    return out
```

```python
import concourse.bass as bass
from concourse import mybir
from contextlib import ExitStack


F32 = mybir.dt.float32
F16 = mybir.dt.float16
I32 = mybir.dt.int32
ALU = mybir.AluOpType
ACT = mybir.ActivationFunctionType
AX = mybir.AxisListType

B, T, D = 4, 1024, 512
P = 128
NC = D // P
Q = 32
NJ = P // Q
G4 = 4 * D
NG = 4 * NC
TB = T // P
U = 8
UB = U * B
ROUNDS = T // U
XCOLS = T * B
XPAD = XCOLS + UB
H_SCALE = 2.0 ** 12
W_TOP = 2.0 ** 14
BIG = 3.0e38


class Sems:

    def __init__(self, nc, ctx, prefix, names):
        self.h = {n: ctx.enter_context(nc.semaphore(prefix + n)) for n in names.split()}

    def __getitem__(self, n):
        return self.h[n]


def load_and_sparsify(nc, m, x, cond, biases1):
    with ExitStack() as ctx:
        s = Sems(nc, ctx, "a_", "x0 x1 x2 x3 cond small id0 tp cpv cps one absd recs recl expd thd zs cum le edge "
                                "hot gat gate2 msk upd recp")
        tp = [ctx.enter_context(nc.psum_tensor(f"tp{i}", [P, 512], F32)) for i in range(4)]
        xin = m.xb_all[:, 0:B * TB * D].rearrange("p (n d) -> p n d", d=D)
        w = [m.scratch[:, i * T:(i + 1) * T] for i in range(14)]
        ax, pi, th, cu = w[0:2], w[2:4], w[4], w[5]
        mk = m.scratch[:, 6 * T:6 * T + T + 1]
        dd, gj, gm = w[8], w[9], w[10:12]
        ones = w[12]
        sm = m.small
        n_tiles = B * NC
        block = ctx.enter_context(nc.Block())

        def col(k, n):
            return sm[:, k * n_tiles + n:k * n_tiles + n + 1]

        def xt(n):
            b, c = divmod(n, NC)
            return m.xa[:, c, 0:XCOLS].rearrange("p (t b) -> p b t", b=B)[:, b, :]

        @block.sync
        def _(sp):
            for b in range(B):
                sp.dma_start(xin[:, b * TB:(b + 1) * TB, :],
                             x[b].rearrange("(n p) d -> p n d", p=P)).then_inc(s[f"x{b}"], 16)
            with nc.allow_non_contiguous_dma(reason="small vectors, features to partitions"):
                for c in range(NC):
                    sp.dma_start(m.cond[:, c, :], cond[:, c * P:(c + 1) * P].rearrange("b p -> p b")).then_inc(s["cond"], 16)
                for dst, src in biases1:
                    sp.dma_start(dst, src).then_inc(s["small"], 16)
            sp.wait_ge(s["small"], 16 * len(biases1))

        @block.gpsimd
        def _(pool):
            nc.gpsimd.memset(m.ident[:], 0.0).then_inc(s["id0"], 1)
            pool.wait_ge(s["id0"], 1)
            nc.gpsimd.affine_select(out=m.ident[:], in_=m.ident[:], compare_op=ALU.not_equal, fill=1.0,
                                    base=0, pattern=[[-1, P]], channel_multiplier=1).then_inc(s["id0"], 1)
            nc.gpsimd.memset(m.eps[:], 1e-8)
            nc.gpsimd.memset(m.xa[:, :, XCOLS:XPAD], 0.0).then_inc(s["one"], 1)
            for n in range(n_tiles):
                pool.wait_ge(s["msk"], n + 1)
                nc.gpsimd.tensor_tensor(xt(n), xt(n), gm[n % 2], ALU.mult).then_inc(s["upd"], 1)

        @block.tensor
        def _(pe):
            pe.wait_ge(s["id0"], 2)
            for n in range(B * TB):
                if n % TB == 0:
                    pe.wait_ge(s[f"x{n // TB}"], 16)
                if n >= 4:
                    pe.wait_ge(s["cpv"] if n % 2 == 0 else s["cps"], (n - 4) // 2 + 1)
                for c in range(NC):
                    last = nc.tensor.transpose(tp[n % 4][:, c * P:(c + 1) * P], xin[:, n, c * P:(c + 1) * P], m.ident[:])
                last.then_inc(s["tp"], 1)

        def out_of(n):
            b, tb = divmod(n, TB)
            dst = m.xa[:, :, 0:XCOLS].rearrange("p c (t b) -> p c b t", b=B)[:, :, b, tb * P:(tb + 1) * P]
            return dst, tp[n % 4][:].rearrange("p (c t) -> p c t", c=NC)

        @block.scalar
        def _(act):
            def absolute(n):
                if n % NC == 0:
                    act.wait_ge(s["cpv"], (n // NC + 1) * TB // 2)
                    act.wait_ge(s["cps"], (n // NC + 1) * TB // 2)
                if n >= 2:
                    act.wait_ge(s["msk"], n - 1)
                nc.scalar.activation(ax[n % 2], xt(n), ACT.Abs, accum_out=col(0, n)).then_inc(s["absd"], 1)

            def exponential(n):
                act.wait_ge(s["recs"], n + 1)
                if n >= 2:
                    act.wait_ge(s["thd"], n - 1)
                nc.scalar.activation(pi[n % 2], ax[n % 2], ACT.Exp, scale=col(2, n), accum_out=col(3, n)).then_inc(s["expd"], 1)

            for b in range(B):
                for n in range(b * TB + 1, (b + 1) * TB, 2):
                    act.wait_ge(s["tp"], n + 1)
                    dst, src = out_of(n)
                    nc.scalar.activation(dst, src, ACT.Copy).then_inc(s["cps"], 1)
                for n in range(b * NC, (b + 1) * NC):
                    absolute(n)
                    if n >= 1:
                        exponential(n - 1)
            exponential(n_tiles - 1)

        @block.vector
        def _(dve):
            nc.vector.memset(ones, 1.0).then_inc(s["zs"], 1)
            nc.vector.memset(mk[:, 0:1], 1.0).then_inc(s["zs"], 1)
            dve.wait_ge(s["zs"], 2)
            dve.wait_ge(s["cond"], 16 * NC)

            def reciprocal(n):
                dve.wait_ge(s["absd"], n + 1)
                nc.vector.reciprocal(col(1, n), col(0, n)).then_inc(s["recl"], 1)
                dve.wait_ge(s["recl"], n + 1)
                nc.vector.tensor_scalar(col(2, n), col(1, n), 2.0, None, ALU.mult).then_inc(s["recs"], 1)

            def tile(n):
                b, c = divmod(n, NC)
                rv = m.cond[:, c, b:b + 1]
                dve.wait_ge(s["expd"], n + 1)
                nc.vector.reciprocal(col(4, n), col(3, n)).then_inc(s["recp"], 1)
                dve.wait_ge(s["recp"], n + 1)
                nc.vector.tensor_scalar(th, pi[n % 2], col(4, n), None, ALU.mult).then_inc(s["thd"], 1)
                dve.wait_ge(s["thd"], n + 1)
                nc.vector.tensor_tensor_scan(cu, ones, th, 0.0, ALU.mult, ALU.add).then_inc(s["cum"], 1)
                dve.wait_ge(s["cum"], n + 1)
                nc.vector.tensor_scalar(mk[:, 1:T + 1], cu, 0.001, rv, ALU.add, ALU.is_le).then_inc(s["le"], 1)
                dve.wait_ge(s["le"], n + 1)
                nc.vector.tensor_tensor(dd, mk[:, 0:T], mk[:, 1:T + 1], ALU.subtract).then_inc(s["hot"], 1)
                dve.wait_ge(s["hot"], n + 1)
                nc.vector.tensor_tensor_reduce(out=gj, in0=dd, in1=ax[n % 2], scale=1.0, scalar=0.0, op0=ALU.mult,
                                               op1=ALU.add, accum_out=col(5, n)).then_inc(s["gat"], 1)
                dve.wait_ge(s["gat"], n + 1)
                nc.vector.scalar_tensor_tensor(col(6, n), mk[:, T:T + 1], BIG, col(5, n), ALU.mult, ALU.add).then_inc(s["gate2"], 1)
                dve.wait_ge(s["gate2"], n + 1)
                if n >= 2:
                    dve.wait_ge(s["upd"], n - 1)
                nc.vector.tensor_scalar(gm[n % 2], ax[n % 2], col(6, n), 1.0, ALU.is_ge, ALU.add).then_inc(s["msk"], 1)

            for b in range(B):
                for n in range(b * TB, (b + 1) * TB, 2):
                    dve.wait_ge(s["tp"], n + 1)
                    dst, src = out_of(n)
                    nc.vector.tensor_copy(dst, src).then_inc(s["cpv"], 1)
                for n in range(b * NC, (b + 1) * NC):
                    reciprocal(n)
                    if n >= 1:
                        tile(n - 1)
            tile(n_tiles - 1)


def lstm(nc, m, tag, xt, wx_sb, w16, wx, wh, bias, rounds=ROUNDS, also_load=()):
    with ExitStack() as ctx:
        s = Sems(nc, ctx, tag, "wh wx ready amax amaxall e2 e2c rcp sc hi lo h0 init xc xw xwt h gif o trg tro s1 pre s1o preo "
                               "next g ifd os fc ig c tc hh hhi xadd zero")
        sbt = lambda n, shape, dt=F32: ctx.enter_context(nc.sbuf_tensor(tag + n, shape, dt))
        pst = lambda n: ctx.enter_context(nc.psum_tensor(tag + n, [P, 512], F32))
        H = sbt("H", [P, 2, NC, 2 * B], F16)
        HH = sbt("HH", [P, U, NC * B])
        XC = sbt("XC", [P, NC, UB])
        XW = sbt("XW", [P, NG, UB])
        GT = sbt("GT", [P, 3 * NC, Q])
        OT = sbt("OT", [P, NC, Q])
        T1 = sbt("T1", [P, 3 * NC, B])
        T1O = sbt("T1O", [P, NC, B])
        PRE = sbt("PRE", [P, 3, NC * B])
        PREO = sbt("PREO", [P, NC * B])
        SG = sbt("SG", [P, NC * B])
        SIF = sbt("SIF", [P, 2, NC * B])
        SO = sbt("SO", [P, NC * B])
        FC = sbt("FC", [P, NC * B])
        IG = sbt("IG", [P, NC * B])
        C = sbt("C", [P, NC * B])
        TC = sbt("TC", [P, NC * B])
        amax, amaxall, e2, rcp, sc, inv = (sbt(n, [P, 1]) for n in ("amax", "amaxall", "e2", "rcp", "sc", "inv"))
        PG, PO, PX = pst("PG"), pst("PO"), pst("PX")
        stage = m.scratch[:, 0:NC * G4].rearrange("p (k n) -> p k n", k=NC)
        block = ctx.enter_context(nc.Block())
        tile_cols = lambda w, k, j, lo, hi: w[:, k, :].rearrange("p (gc j i) -> p gc j i", j=NJ, i=Q)[:, lo:hi, j, :]
        by_unit = lambda a: a.rearrange("p (c b) -> p c b", b=B)

        def gates_first(dst, src, sp, sem):
            v = src.rearrange("(k p) n -> p k n", p=P)
            sp.dma_start(dst[:, :, 0:D], v[:, :, 3 * D:]).then_inc(sem, 16)
            sp.dma_start(dst[:, :, D:], v[:, :, 0:3 * D]).then_inc(sem, 16)

        @block.sync
        def _(sp):
            gates_first(stage, wh, sp, s["wh"])
            gates_first(wx_sb, wx, sp, s["wx"])
            for dst, src in also_load:
                sp.dma_start(dst, src).then_inc(s["next"], 16)
            if also_load:
                sp.wait_ge(s["next"], 16 * len(also_load))

        @block.gpsimd
        def _(pool):
            nc.gpsimd.memset(HH[:], 0.0).then_inc(s["xadd"], 1)
            nc.gpsimd.tensor_copy(XC[:], xt[:, :, 0:UB]).then_inc(s["xc"], 1)
            pool.wait_ge(s["amax"], 1)
            nc.gpsimd.partition_all_reduce(amaxall[:], amax[:], P, bass.bass_isa.ReduceOp.max).then_inc(s["amaxall"], 1)
            with pool.Fori(0, rounds) as r:
                pool.wait_ge(s["xw"], r + 1)
                nc.gpsimd.tensor_copy(XC[:], xt[:, :, bass.ds((r + 1) * UB, UB)]).then_inc(s["xc"], 1)
                pool.wait_ge(s["h"], r * U + (U + 1))
                for c in range(NC):
                    here = xt[:, c, bass.ds(r * UB, UB)].rearrange("p (u b) -> p u b", b=B)
                    last = nc.gpsimd.tensor_tensor(here, here, HH[:].rearrange("p u (c b) -> p u c b", b=B)[:, :, c, :], ALU.add)
                last.then_inc(s["xadd"], 1)

        @block.tensor
        def _(pe):
            def x_product(n):
                k, half = divmod(n, 2)
                lo, hi = half * (NG // 2), (half + 1) * (NG // 2)
                for j in range(NJ):
                    last = nc.tensor.matmul(PX[Q * j:Q * j + UB, lo * Q:hi * Q], XC[:, k, :], tile_cols(wx_sb, k, j, lo, hi),
                                            start=(n == 0), stop=(n == U - 1), skip_group_check=True)
                return last

            pe.wait_ge(s["wx"], 32)
            pe.wait_ge(s["xc"], 1)
            for n in range(U):
                last = x_product(n)
            pe.wait_ge(s["wh"], 32)
            for k in range(NC):
                for j in range(NJ):
                    last = nc.tensor.matmul(PX[Q * j:Q * j + B, :], m.cond[:, k, :], tile_cols(stage, k, j, 0, NG),
                                            start=False, stop=True, skip_group_check=True)
            last.then_inc(s["xw"], 1)
            pe.wait_ge(s["zero"], 1)
            pe.wait_ge(s["lo"], NC * NJ)
            pe.wait_ge(s["hi"], NC)
            with pe.Fori(0, rounds) as r:
                for u in range(U):
                    now = pe.snap(r * U + (u + 1))
                    pe.wait_ge(s["h"], now)
                    for bank, lo, hi, done in ((PG, 0, 3 * D // NJ, "gif"), (PO, 3 * D // NJ, D, "o")):
                        for k in range(NC):
                            for part in range(2):
                                for j in range(NJ):
                                    last = nc.tensor.matmul(bank[Q * j:Q * j + 2 * B, 0:hi - lo], H[:, u % 2, k, :],
                                                            w16[:, part, k, j, lo:hi], start=(k == 0 and part == 0),
                                                            stop=(k == NC - 1 and part == 1))
                        last.then_inc(s[done], 1)
                    if u == 0:
                        pe.wait_ge(s["xc"], r + 2)
                        pe.wait_ge(s["xwt"], r + 1)
                    last = x_product(u)
                last.then_inc(s["xw"], 1)

        @block.scalar
        def _(act):
            act.wait_ge(s["wh"], 32)
            act.wait_ge(s["sc"], 1)
            for k in range(NC):
                for j in range(NJ):
                    last = nc.scalar.activation(w16[:, 0, k, j, :].rearrange("p (gc i) -> p gc i", i=Q),
                                                tile_cols(stage, k, j, 0, NG), ACT.Copy, scale=sc[:])
                last.then_inc(s["hi"], 1)
            with act.Fori(0, rounds) as r:
                for u in range(U):
                    now = act.snap(r * U + (u + 1))
                    act.wait_ge(s["pre"], now)
                    nc.scalar.activation(SG[:], PRE[:, 0, :], ACT.Tanh).then_inc(s["g"], 1)
                    nc.scalar.activation(SIF[:], PRE[:, 1:3, :], ACT.Sigmoid).then_inc(s["ifd"], 1)
                    act.wait_ge(s["c"], now)
                    nc.scalar.activation(TC[:], C[:], ACT.Tanh).then_inc(s["tc"], 1)
                    act.wait_ge(s["preo"], now)
                    nc.scalar.activation(SO[:], PREO[:], ACT.Sigmoid).then_inc(s["os"], 1)

        @block.vector
        def _(dve):
            for bank in (PG, PO):
                last = nc.vector.memset(bank[:], 0.0)
            nc.vector.memset(C[:], 0.0).then_inc(s["zero"], 1)
            dve.wait_ge(s["wh"], 32)
            nc.vector.tensor_reduce(amax[:], stage, AX.XY, ALU.max, apply_absolute_value=True).then_inc(s["amax"], 1)
            dve.wait_ge(s["amaxall"], 1)
            nc.vector.tensor_scalar(e2[:].bitcast(I32), amaxall[:].bitcast(I32), 0x7F800000, None, ALU.bitwise_and).then_inc(s["e2"], 1)
            dve.wait_ge(s["e2"], 1)
            nc.vector.tensor_scalar(e2[:], e2[:], 2.0 ** -80, 2.0 ** 80, ALU.max, ALU.min).then_inc(s["e2c"], 1)
            dve.wait_ge(s["e2c"], 1)
            nc.vector.reciprocal(rcp[:], e2[:]).then_inc(s["rcp"], 1)
            dve.wait_ge(s["rcp"], 1)
            nc.vector.tensor_scalar(sc[:], rcp[:], W_TOP, None, ALU.mult).then_inc(s["sc"], 1)
            nc.vector.tensor_scalar(inv[:], e2[:], 1.0 / (W_TOP * H_SCALE), None, ALU.mult).then_inc(s["rcp"], 1)
            dve.wait_ge(s["sc"], 1)
            for k in range(NC):
                dve.wait_ge(s["hi"], k + 1)
                for j in range(NJ):
                    view = lambda part: w16[:, part, k, j, :].rearrange("p (gc i) -> p gc i", i=Q)
                    nc.vector.scalar_tensor_tensor(view(1), tile_cols(stage, k, j, 0, NG), sc[:], view(0),
                                                   ALU.mult, ALU.subtract).then_inc(s["lo"], 1)
            dve.wait_ge(s["zero"], 1)
            dve.wait_ge(s["rcp"], 2)
            nc.vector.memset(H[:], 0.0).then_inc(s["h"], 1)
            sums = (("s1", "pre"), ("s1o", "preo"))
            with dve.Fori(0, rounds) as r:
                for u in range(U):
                    now = dve.snap(r * U + (u + 1))
                    if u == 0:
                        dve.wait_ge(s["xw"], r + 1)
                        nc.vector.transpose(XW[:].rearrange("p g n -> p (g n)"), PX[:]).then_inc(s["xwt"], 1)
                        dve.wait_ge(s["xwt"], r + 1)
                        nc.vector.tensor_tensor(XW[:], XW[:], bias[:].rearrange("p (g o) -> p g o", o=1).broadcast_to([P, NG, UB]),
                                                ALU.add).then_inc(s["init"], 1)

                    def pre_activation(t, xw, part, out, group):
                        nc.vector.scalar_tensor_tensor(part, t[:, :, B:2 * B], inv[:], xw, ALU.mult, ALU.add).then_inc(s[sums[group][0]], 1)
                        dve.wait_ge(s[sums[group][0]], now)
                        nc.vector.scalar_tensor_tensor(out, t[:, :, 0:B], inv[:], part, ALU.mult, ALU.add).then_inc(s[sums[group][1]], 1)

                    xw = XW[:, :, u * B:(u + 1) * B]
                    dve.wait_ge(s["gif"], now)
                    nc.vector.transpose(GT[:].rearrange("p g n -> p (g n)"), PG[:, 0:3 * NC * Q]).then_inc(s["trg"], 1)
                    if u == 0:
                        dve.wait_ge(s["init"], r + 1)
                    dve.wait_ge(s["trg"], now)
                    pre_activation(GT, xw[:, 0:3 * NC, :], T1[:], PRE[:].rearrange("p g (c b) -> p (g c) b", b=B), 0)
                    dve.wait_ge(s["o"], now)
                    nc.vector.transpose(OT[:].rearrange("p g n -> p (g n)"), PO[:, 0:NC * Q]).then_inc(s["tro"], 1)
                    dve.wait_ge(s["ifd"], now)
                    nc.vector.tensor_tensor(FC[:], SIF[:, 1, :], C[:], ALU.mult).then_inc(s["fc"], 1)
                    dve.wait_ge(s["g"], now)
                    nc.vector.tensor_tensor(IG[:], SIF[:, 0, :], SG[:], ALU.mult).then_inc(s["ig"], 1)
                    dve.wait_ge(s["fc"], now)
                    dve.wait_ge(s["ig"], now)
                    nc.vector.tensor_tensor(C[:], FC[:], IG[:], ALU.add).then_inc(s["c"], 1)
                    dve.wait_ge(s["tro"], now)
                    pre_activation(OT, xw[:, 3 * NC:, :], T1O[:], by_unit(PREO[:]), 1)
                    dve.wait_ge(s["tc"], now)
                    dve.wait_ge(s["os"], now)
                    if u == 0:
                        dve.wait_ge(s["xadd"], r + 1)
                    nxt = H[:, (u + 1) % 2]
                    nc.vector.tensor_tensor(HH[:, u, :], SO[:], TC[:], ALU.mult).then_inc(s["hh"], 1)
                    nc.vector.scalar_tensor_tensor(nxt[:, :, 0:B], by_unit(SO[:]), H_SCALE, by_unit(TC[:]), ALU.mult, ALU.mult).then_inc(s["hhi"], 1)
                    dve.wait_ge(s["hh"], now)
                    dve.wait_ge(s["hhi"], now)
                    nc.vector.scalar_tensor_tensor(nxt[:, :, B:2 * B], by_unit(HH[:, u, :]), H_SCALE, nxt[:, :, 0:B],
                                                   ALU.mult, ALU.subtract).then_inc(s["h"], 1)
            dve.wait_ge(s["xw"], rounds + 1)
            dve.wait_ge(s["xadd"], rounds + 1)


def gated_scan(nc, m, biases2, pad):
    with ExitStack() as ctx:
        s = Sems(nc, ctx, "g_", "tw cw z f i gs rg fn inm ni ln one lc ex0 ex1 sn hid sum out small")
        sbt = lambda n, shape, dt=F32: ctx.enter_context(nc.sbuf_tensor("g_" + n, shape, dt))
        banks = [ctx.enter_context(nc.psum_tensor(f"g_z{i}", [P, 512], F32)) for i in range(8)]
        TBB = P * B
        natural = m.natural_weights()
        wt = m.scratch[:, 0:3 * NC * D].rearrange("p (w k h) -> p w k h", w=3, k=NC)
        F = sbt("F", [P, 2, TBB])
        I = sbt("I", [P, 2, TBB])
        GS = sbt("GS", [P, TBB])
        LC = sbt("LC", [P, 2, T + 1])
        ones = sbt("ones", [P, 1])
        ni_buf = [m.scratch[:, 3 * NC * D + i * XCOLS:3 * NC * D + (i + 1) * XCOLS] for i in range(2)]
        items = [(c, n) for c in range(NC + 1) for n in range(TB)]
        block = ctx.enter_context(nc.Block())
        row = lambda a, b: a.rearrange("p (t b) -> p b t", b=B)[:, b, :]
        lr = lambda c: m.xb[:, c, 0:XCOLS]

        def blocks_and_scans(on_block, on_first, on_second):
            for c, n in items:
                if c < NC:
                    on_block(c, n, c * TB + n)
                if c > 0:
                    q = (c - 1) * B + n // 2
                    (on_second if n % 2 else on_first)(c - 1, n // 2, q)

        @block.sync
        def _(sp):
            with nc.allow_non_contiguous_dma(reason="small vectors, features to partitions"):
                for dst, src in biases2:
                    sp.dma_start(dst, src).then_inc(s["small"], 16)
            sp.wait_ge(s["small"], 16 * len(biases2))

        @block.gpsimd
        def _(pool):
            nc.gpsimd.memset(pad, 0.0)
            for q in range(NC * B):
                c, b = divmod(q, B)
                pool.wait_ge(s["sum"], q + 1)
                nc.gpsimd.tensor_tensor(row(lr(c), b), row(lr(c), b), row(m.xa[:, c, 0:XCOLS], b), ALU.add).then_inc(s["out"], 1)

        @block.tensor
        def _(pe):
            for n in range(3 * NC):
                w, k = divmod(n, NC)
                if n >= 8:
                    pe.wait_ge(s["cw"], n - 7)
                for h in range(NC):
                    last = nc.tensor.transpose(banks[n % 8][:, h * P:(h + 1) * P], natural[:, w * NC + h, k * P:(k + 1) * P], m.ident[:])
                last.then_inc(s["tw"], 1)
            pe.wait_ge(s["cw"], 3 * NC)
            for n in range(NC * TB):
                c, blk = divmod(n, TB)
                if n >= 2:
                    pe.wait_ge(s["f"], n - 1)
                    pe.wait_ge(s["i"], n - 1)
                    pe.wait_ge(s["ni"], n - 1)
                for w in range(3):
                    for k in range(NC):
                        last = nc.tensor.matmul(banks[w * 2 + n % 2][:], wt[:, w, k, c * P:(c + 1) * P],
                                                m.xa[:, k, blk * TBB:(blk + 1) * TBB], start=(k == 0), stop=(k == NC - 1))
                    last.then_inc(s["z"], 1)

        @block.scalar
        def _(act):
            act.wait_ge(s["small"], 16 * len(biases2))

            def gates(c, blk, n):
                act.wait_ge(s["z"], 3 * n + 1)
                if n >= 2:
                    act.wait_ge(s["ni"], n - 1)
                nc.scalar.activation(F[:, n % 2], banks[n % 2][:], ACT.Sigmoid, bias=m.bias2[:, 0, c:c + 1]).then_inc(s["f"], 1)
                act.wait_ge(s["z"], 3 * n + 2)
                nc.scalar.activation(I[:, n % 2], banks[2 + n % 2][:], ACT.Sigmoid, bias=m.bias2[:, 1, c:c + 1]).then_inc(s["i"], 1)
                act.wait_ge(s["fn"], n + 1)
                nc.scalar.activation(lr(c)[:, blk * TBB:(blk + 1) * TBB], F[:, n % 2], ACT.Ln, bias=m.eps[:]).then_inc(s["ln"], 1)

            def exponentials(c, b, q):
                act.wait_ge(s["lc"], q + 1)
                lc = LC[:, q % 2]
                nc.scalar.activation(row(lr(c), b), lc[:, 0:T], ACT.Exp, scale=-1.0, bias=lc[:, T:T + 1]).then_inc(s["ex0"], 1)
                act.wait_ge(s["ex0"], q + 1)
                nc.scalar.activation(lc[:, 1:T + 1], lc[:, 1:T + 1], ACT.Exp).then_inc(s["ex1"], 1)

            blocks_and_scans(gates, exponentials, lambda c, b, q: None)

        @block.vector
        def _(dve):
            nc.vector.memset(ones[:], 1.0).then_inc(s["one"], 1)
            nc.vector.memset(LC[:, :, 0:1], 0.0).then_inc(s["one"], 1)
            for n in range(3 * NC):
                w, k = divmod(n, NC)
                dve.wait_ge(s["tw"], n + 1)
                nc.vector.tensor_copy(wt[:, w, k, :], banks[n % 8][:]).then_inc(s["cw"], 1)
            dve.wait_ge(s["one"], 2)
            dve.wait_ge(s["small"], 16 * len(biases2))
            running = ones[:].broadcast_to([P, T])

            def ratios(c, blk, n):
                f, i = F[:, n % 2], I[:, n % 2]
                dve.wait_ge(s["f"], n + 1)
                dve.wait_ge(s["i"], n + 1)
                nc.vector.scalar_tensor_tensor(GS[:], f, 1e-8, i, ALU.add, ALU.add).then_inc(s["gs"], 1)
                dve.wait_ge(s["gs"], n + 1)
                nc.vector.reciprocal(GS[:], GS[:]).then_inc(s["rg"], 1)
                dve.wait_ge(s["rg"], n + 1)
                nc.vector.tensor_tensor(f, f, GS[:], ALU.mult).then_inc(s["fn"], 1)
                nc.vector.tensor_tensor(i, i, GS[:], ALU.mult).then_inc(s["inm"], 1)
                dve.wait_ge(s["inm"], n + 1)
                dve.wait_ge(s["z"], 3 * n + 3)
                if blk == 0 and c >= 2:
                    dve.wait_ge(s["hid"], (c - 1) * B)
                nc.vector.scalar_tensor_tensor(ni_buf[c % 2][:, blk * TBB:(blk + 1) * TBB], banks[4 + n % 2][:],
                                               m.bias2[:, 2, c:c + 1], i, ALU.add, ALU.mult).then_inc(s["ni"], 1)

            def log_scan(c, b, q):
                dve.wait_ge(s["ln"], (c + 1) * TB)
                if q >= 2:
                    dve.wait_ge(s["sum"], q - 1)
                nc.vector.tensor_tensor_scan(LC[:, q % 2, 1:T + 1], running, row(lr(c), b), 0.0, ALU.mult, ALU.add).then_inc(s["lc"], 1)

            def hidden_scan(c, b, q):
                ni = row(ni_buf[c % 2], b)
                dve.wait_ge(s["ni"], (c + 1) * TB)
                dve.wait_ge(s["ex0"], q + 1)
                nc.vector.tensor_tensor(ni, ni, row(lr(c), b), ALU.mult).then_inc(s["sn"], 1)
                dve.wait_ge(s["sn"], q + 1)
                nc.vector.tensor_tensor_scan(row(lr(c), b), running, ni, 0.0, ALU.mult, ALU.add).then_inc(s["hid"], 1)
                dve.wait_ge(s["hid"], q + 1)
                dve.wait_ge(s["ex1"], q + 1)
                nc.vector.scalar_tensor_tensor(row(lr(c), b), LC[:, q % 2, 1:T + 1], m.cond[:, c, b:b + 1], row(lr(c), b),
                                               ALU.mult, ALU.add).then_inc(s["sum"], 1)

            blocks_and_scans(ratios, log_scan, hidden_scan)


def store(nc, m, out):
    with ExitStack() as ctx:
        s = Sems(nc, ctx, "s_", "tp cpv cps out")
        tp = [ctx.enter_context(nc.psum_tensor(f"s_tp{i}", [P, 512], F32)) for i in range(8)]
        xo = m.xa_all[:, 0:B * TB * D].rearrange("p (n d) -> p n d", d=D)
        block = ctx.enter_context(nc.Block())

        @block.tensor
        def _(pe):
            for n in range(B * TB):
                b, tb = divmod(n, TB)
                if n >= 8:
                    pe.wait_ge(s["cpv"] if n % 2 == 0 else s["cps"], (n - 8) // 2 + 1)
                for c in range(NC):
                    src = m.xb[:, c, 0:XCOLS].rearrange("p (t b) -> p b t", b=B)[:, b, tb * P:(tb + 1) * P]
                    last = nc.tensor.transpose(tp[n % 8][:, c * P:(c + 1) * P], src, m.ident[:])
                last.then_inc(s["tp"], 1)

        @block.vector
        def _(dve):
            for n in range(0, B * TB, 2):
                dve.wait_ge(s["tp"], n + 1)
                nc.vector.tensor_copy(xo[:, n, :], tp[n % 8][:]).then_inc(s["cpv"], 1)

        @block.scalar
        def _(act):
            for n in range(1, B * TB, 2):
                act.wait_ge(s["tp"], n + 1)
                nc.scalar.activation(xo[:, n, :], tp[n % 8][:], ACT.Copy).then_inc(s["cps"], 1)

        @block.sync
        def _(sp):
            for n in range(0, B * TB, 2):
                b, tb = divmod(n, TB)
                sp.wait_ge(s["cpv"], n // 2 + 1)
                sp.wait_ge(s["cps"], n // 2 + 1)
                sp.dma_start(out[b, tb * P:(tb + 2) * P, :].rearrange("(n p) d -> p n d", p=P), xo[:, n:n + 2, :]).then_inc(s["out"], 16)
            sp.wait_ge(s["out"], 16 * (B * TB // 2))


class Memory:

    def __init__(self, nc, ctx):
        sbt = lambda n, shape: ctx.enter_context(nc.sbuf_tensor(n, shape, F32))
        self.xa_all = sbt("xa", [P, NC * XPAD])
        self.xb_all = sbt("xb", [P, NC * XPAD])
        self.scratch = sbt("scratch", [P, 14 * T])
        self.xa = self.xa_all[:].rearrange("p (c n) -> p c n", c=NC)
        self.xb = self.xb_all[:].rearrange("p (c n) -> p c n", c=NC)
        self.ident = sbt("ident", [P, P])
        self.cond = sbt("cond", [P, NC, B])
        self.bias1 = sbt("bias1", [P, NG])
        self.bias3 = sbt("bias3", [P, NG])
        self.bias2 = sbt("bias2", [P, 3, NC])
        self.eps = sbt("eps", [P, 1])
        self.small = sbt("small", [P, 7 * B * NC])

    def natural_weights(self):
        return self.scratch[:, NC * G4:NC * G4 + 3 * NC * D].rearrange("p (n d) -> p n d", d=D)

    def lstm_weights(self, region):
        half = NC * G4
        fp32 = region[:, 0:half].rearrange("p (k n) -> p k n", k=NC)
        parts = region[:, half:2 * half].bitcast(F16).rearrange("p (s k j n) -> p s k j n", s=2, k=NC, j=NJ)
        return fp32, parts


def program(nc, x, cond, wx1, wh1, b1, wf, bf, wi, bi, wh, bh, wx3, wh3, b3, out):
    with ExitStack() as ctx:
        m = Memory(nc, ctx)

        def lstm_bias(dst, b):
            v = b.rearrange("(g p) -> p g", p=P)
            return [(dst[:, 0:NC], v[:, 3 * NC:]), (dst[:, NC:], v[:, 0:3 * NC])]

        units = lambda b: b.rearrange("(c p) -> p c", p=P)
        load_and_sparsify(nc, m, x, cond, lstm_bias(m.bias1, b1) + lstm_bias(m.bias3, b3))
        fp32, parts = m.lstm_weights(m.xb_all)
        natural = m.natural_weights()
        lstm(nc, m, "p_", m.xa, fp32, parts, wx1, wh1, m.bias1,
             also_load=[(natural[:, w * NC:(w + 1) * NC, :], a.rearrange("(h p) d -> p h d", p=P)) for w, a in enumerate((wf, wi, wh))])
        gated_scan(nc, m, [(m.bias2[:, w, :], units(b)) for w, b in enumerate((bf, bi, bh))], m.xb[:, :, XCOLS:XPAD])
        fp32, parts = m.lstm_weights(m.xa_all)
        lstm(nc, m, "q_", m.xb, fp32, parts, wx3, wh3, m.bias3)
        store(nc, m, out)


_INS = ['x', 'cond_1024', 'L1_cond_Wx', 'L1_cond_Wh', 'L1_cond_b', 'L2_cond_W_f', 'L2_cond_b_f', 'L2_cond_W_i',
        'L2_cond_b_i', 'L2_cond_W_h', 'L2_cond_b_h', 'L3_cond_Wx', 'L3_cond_Wh', 'L3_cond_b']


def kernel(**inputs):
    import numpy as _np
    import concourse.bacc as _bacc
    from concourse import mybir as _mybir
    from concourse.bass_utils import run_bass_kernel_spmd as _run

    nc = _bacc.Bacc("TRN2", target_bir_lowering=False, num_devices=1)
    arrays, args = {}, []
    for name in _INS:
        a = _np.ascontiguousarray(inputs[name])
        arrays[f"in_{name}_dram"] = a
        args.append(nc.dram_tensor(f"in_{name}_dram", a.shape, _mybir.dt.from_np(a.dtype), kind="ExternalInput").ap())
    args.append(nc.dram_tensor("out_0_dram", (B, T, D), _mybir.dt.float32, kind="ExternalOutput").ap())
    program(nc, *args)
    r = _run(nc, [arrays], core_ids=[0])
    return r.results[0]["out_0_dram"]
```

```python
import concourse.bass as bass
from concourse import mybir
from contextlib import ExitStack


F32 = mybir.dt.float32
F16 = mybir.dt.float16
I32 = mybir.dt.int32
ALU = mybir.AluOpType
ACT = mybir.ActivationFunctionType
AX = mybir.AxisListType

B, T, D = 4, 1024, 512
P = 128
NC = D // P
Q = 32
NJ = P // Q
G4 = 4 * D
NG = 4 * NC
TB = T // P
U = 8
UB = U * B
ROUNDS = T // U
XCOLS = T * B
XPAD = XCOLS + UB
USUAL = (2.0 ** -6, 1.0)
H_SCALE = 2.0 ** 12
W_TOP = 2.0 ** 14
BIG = 3.0e38


class Sems:

    def __init__(self, nc, ctx, prefix, names):
        self.h = {n: ctx.enter_context(nc.semaphore(prefix + n)) for n in names.split()}

    def __getitem__(self, n):
        return self.h[n]


def gates_first(m_dst, src, sp, sem, chunks=range(NC)):
    a, b = chunks[0], chunks[-1] + 1
    v = src.rearrange("(k p) n -> p k n", p=P)
    sp.dma_start(m_dst[:, a:b, 0:D], v[:, a:b, 3 * D:]).then_inc(sem, 16)
    sp.dma_start(m_dst[:, a:b, D:], v[:, a:b, 0:3 * D]).then_inc(sem, 16)


def load_and_sparsify(nc, m, x, cond, lstm_loads):
    with ExitStack() as ctx:
        s = Sems(nc, ctx, "a_", "x0 x1 cond weights id0 tp cpv cps one absd recs recl expd thd zs cum le "
                                "hot gat gate2 msk upd recp")
        tp = [ctx.enter_context(nc.psum_tensor(f"tp{i}", [P, 512], F32)) for i in range(8)]
        PART = 4
        ring = m.scratch[:, 0:2 * PART * D].rearrange("p (n d) -> p n d", d=D)
        w = [m.scratch[:, 2 * PART * D + i * T:2 * PART * D + (i + 1) * T] for i in range(8)]
        ax, pi, dd, gm = w[0:4], w[4:6], w[6], w[7]
        mk = m.scratch[:, 2 * PART * D + 8 * T:2 * PART * D + 9 * T + 1]
        sm = m.small
        n_tiles = B * NC
        block = ctx.enter_context(nc.Block())

        def col(k, n):
            return sm[:, k * n_tiles + n:k * n_tiles + n + 1]

        def xt(n):
            b, c = divmod(n, NC)
            return m.xa[:, c, 0:XCOLS].rearrange("p (t b) -> p b t", b=B)[:, b, :]

        @block.sync
        def _(sp):
            for k in range(B * TB // PART):
                if k >= 2:
                    sp.wait_ge(s["tp"], PART * (k - 1))
                b, half = divmod(k, TB // PART)
                sp.dma_start(ring[:, (k % 2) * PART:(k % 2 + 1) * PART, :],
                             x[b, half * PART * P:(half + 1) * PART * P, :].rearrange("(n p) d -> p n d", p=P)).then_inc(s[f"x{k % 2}"], 16)
                if k == 1:
                    with nc.allow_non_contiguous_dma(reason="small vectors, features to partitions"):
                        for c in range(NC):
                            sp.dma_start(m.cond[:, c, :], cond[:, c * P:(c + 1) * P].rearrange("b p -> p b")).then_inc(s["cond"], 16)
            for dst, src in lstm_loads:
                gates_first(dst, src, sp, s["weights"])
            sp.wait_ge(s["weights"], 32 * len(lstm_loads))

        @block.gpsimd
        def _(pool):
            nc.gpsimd.memset(m.ident[:], 0.0).then_inc(s["id0"], 1)
            pool.wait_ge(s["id0"], 1)
            nc.gpsimd.affine_select(out=m.ident[:], in_=m.ident[:], compare_op=ALU.not_equal, fill=1.0,
                                    base=0, pattern=[[-1, P]], channel_multiplier=1).then_inc(s["id0"], 1)
            nc.gpsimd.memset(m.eps[:], 1e-8)
            nc.gpsimd.memset(m.xa[:, :, XCOLS:XPAD], 0.0).then_inc(s["one"], 1)
            for i in range(2, n_tiles + 3):
                if i - 2 < n_tiles:
                    n = i - 2
                    pool.wait_ge(s["le"], n + 1)
                    if n >= 1:
                        pool.wait_ge(s["gat"], n)
                    nc.gpsimd.tensor_tensor(dd, mk[:, 0:T], mk[:, 1:T + 1], ALU.subtract).then_inc(s["hot"], 1)
                if i >= 3:
                    n = i - 3
                    pool.wait_ge(s["msk"], n + 1)
                    nc.gpsimd.tensor_tensor(xt(n), xt(n), gm, ALU.mult).then_inc(s["upd"], 1)

        @block.tensor
        def _(pe):
            pe.wait_ge(s["id0"], 2)
            for n in range(B * TB):
                if n % PART == 0:
                    k = n // PART
                    pe.wait_ge(s[f"x{k % 2}"], 16 * (k // 2 + 1))
                if n >= 8:
                    pe.wait_ge(s["cpv"] if n % 2 == 0 else s["cps"], (n - 8) // 2 + 1)
                for c in range(NC):
                    last = nc.tensor.transpose(tp[n % 8][:, c * P:(c + 1) * P], ring[:, n % (2 * PART), c * P:(c + 1) * P], m.ident[:])
                last.then_inc(s["tp"], 1)

        def out_of(n):
            b, tb = divmod(n, TB)
            dst = m.xa[:, :, 0:XCOLS].rearrange("p c (t b) -> p c b t", b=B)[:, :, b, tb * P:(tb + 1) * P]
            return dst, tp[n % 8][:].rearrange("p (c t) -> p c t", c=NC)

        @block.scalar
        def _(act):
            def absolute(n):
                if n % NC == 0:
                    act.wait_ge(s["cpv"], (n // NC + 1) * TB // 2)
                    act.wait_ge(s["cps"], (n // NC + 1) * TB // 2)
                if n >= 4:
                    act.wait_ge(s["msk"], n - 3)
                nc.scalar.activation(ax[n % 4], xt(n), ACT.Abs, accum_out=col(0, n)).then_inc(s["absd"], 1)

            def exponential(n):
                act.wait_ge(s["recs"], n + 1)
                if n >= 2:
                    act.wait_ge(s["le"], n - 1)
                nc.scalar.activation(pi[n % 2], ax[n % 4], ACT.Exp, scale=col(2, n), accum_out=col(3, n)).then_inc(s["expd"], 1)

            def thresholds(n):
                act.wait_ge(s["recp"], n + 1)
                nc.scalar.activation(pi[n % 2], pi[n % 2], ACT.Copy, scale=col(4, n)).then_inc(s["thd"], 1)

            for i in range(n_tiles + 2):
                b, c = divmod(i, NC)
                if c == 0 and b < B:
                    for n in range(b * TB + 1, (b + 1) * TB, 2):
                        act.wait_ge(s["tp"], n + 1)
                        dst, src = out_of(n)
                        nc.scalar.activation(dst, src, ACT.Copy).then_inc(s["cps"], 1)
                if i >= 2:
                    thresholds(i - 2)
                if i < n_tiles:
                    absolute(i)
                if 1 <= i <= n_tiles:
                    exponential(i - 1)

        @block.vector
        def _(dve):
            nc.vector.memset(m.one[:], 1.0).then_inc(s["zs"], 1)
            nc.vector.memset(mk[:, 0:1], 1.0).then_inc(s["zs"], 1)
            dve.wait_ge(s["zs"], 2)
            running = m.one[:].broadcast_to([P, T])

            def reciprocal(n):
                dve.wait_ge(s["absd"], n + 1)
                nc.vector.reciprocal(col(1, n), col(0, n)).then_inc(s["recl"], 1)
                dve.wait_ge(s["recl"], n + 1)
                nc.vector.tensor_scalar(col(2, n), col(1, n), 2.0, None, ALU.mult).then_inc(s["recs"], 1)

            def reciprocal_pi(n):
                dve.wait_ge(s["expd"], n + 1)
                nc.vector.reciprocal(col(4, n), col(3, n)).then_inc(s["recp"], 1)

            def cumulate(n):
                b, c = divmod(n, NC)
                dve.wait_ge(s["thd"], n + 1)
                nc.vector.tensor_tensor_scan(pi[n % 2], running, pi[n % 2], 0.0, ALU.mult, ALU.add).then_inc(s["cum"], 1)
                dve.wait_ge(s["cum"], n + 1)
                nc.vector.tensor_scalar(mk[:, 1:T + 1], pi[n % 2], 0.001, m.cond[:, c, b:b + 1], ALU.add, ALU.is_le).then_inc(s["le"], 1)

            def mask(n):
                dve.wait_ge(s["hot"], n + 1)
                nc.vector.tensor_tensor_reduce(out=dd, in0=dd, in1=ax[n % 4], scale=1.0, scalar=0.0, op0=ALU.mult,
                                               op1=ALU.add, accum_out=col(5, n)).then_inc(s["gat"], 1)
                dve.wait_ge(s["gat"], n + 1)
                nc.vector.scalar_tensor_tensor(col(6, n), mk[:, T:T + 1], BIG, col(5, n), ALU.mult, ALU.add).then_inc(s["gate2"], 1)
                dve.wait_ge(s["gate2"], n + 1)
                if n >= 1:
                    dve.wait_ge(s["upd"], n)
                nc.vector.tensor_scalar(gm, ax[n % 4], col(6, n), 1.0, ALU.is_ge, ALU.add).then_inc(s["msk"], 1)

            dve.wait_ge(s["cond"], 16 * NC)
            for i in range(n_tiles + 3):
                b, c = divmod(i, NC)
                if c == 0 and b < B:
                    for n in range(b * TB, (b + 1) * TB, 2):
                        dve.wait_ge(s["tp"], n + 1)
                        dst, src = out_of(n)
                        nc.vector.tensor_copy(dst, src).then_inc(s["cpv"], 1)
                if i >= 3:
                    mask(i - 3)
                if i < n_tiles:
                    reciprocal(i)
                if 2 <= i < n_tiles + 2:
                    cumulate(i - 2)
                if 1 <= i <= n_tiles:
                    reciprocal_pi(i - 1)


def lstm(nc, m, tag, xt, weights, wh, b, wh_there, rounds=ROUNDS, also_load=()):
    with ExitStack() as ctx:
        s = Sems(nc, ctx, tag, "bias trg0 preg us usual xr sel0 sel1 sel wh wx ready amax amaxall e2 e2c rcp sc hi lo h0 init xc xw xwt h gif o trg tro s1 pre s1o preo "
                               "next g ifd os fc ig c tc hh hhi xadd zero")
        sbt = lambda n, shape, dt=F32: ctx.enter_context(nc.sbuf_tensor(tag + n, shape, dt))
        pst = lambda n: ctx.enter_context(nc.psum_tensor(tag + n, [P, 512], F32))
        H = sbt("H", [P, 2, NC, 2 * B], F16)
        HH = sbt("HH", [P, U, NC * B])
        XC = sbt("XC", [P, NC, UB])
        XR = sbt("XR", [P, NG * Q])
        bias = sbt("bias", [P, NG * Q])
        SEL = sbt("SEL", [P, U, NJ, 2 * B])
        GT = sbt("GT", [P, 3 * NC, Q])
        OT = sbt("OT", [P, NC, Q])
        SIF = sbt("SIF", [P, 2, NC * B])
        SO = sbt("SO", [P, NC * B])
        IGFC = sbt("IGFC", [P, 2, NC * B])
        one_sig = sbt("one_sig", [P, 1])
        low, one_less = sbt("low", [P, 1]), sbt("one_less", [P, 1])
        usual_i = sbt("usual_i", [P, 1], I32)
        outv, amax, amaxall, e2, rcp, sc, inv = (sbt(n, [P, 1]) for n in ("outv", "amax", "amaxall", "e2", "rcp", "sc", "inv"))
        PG, PO, PX = pst("PG"), pst("PO"), pst("PX")
        PREG = pst("PREG")[:, 0:NC * B]
        PRE = pst("PRE")[:, 0:2 * NC * B]
        PREO = pst("PREO")[:, 0:NC * B]
        GC = pst("GC")[:, 0:2 * NC * B]
        G, C = GC[:, 0:NC * B], GC[:, NC * B:]
        TC = pst("TC")[:, 0:NC * B]
        wx_sb, stage, w16 = weights
        wh_loads = 32 * (NC - wh_there)
        block = ctx.enter_context(nc.Block())
        tile_cols = lambda w, k, j, lo, hi: w[:, k, :].rearrange("p (gc j i) -> p gc j i", j=NJ, i=Q)[:, lo:hi, j, :]
        by_unit = lambda a: a.rearrange("p (c b) -> p c b", b=B)

        def wh_arrived(eng):
            if wh_loads:
                eng.wait_ge(s["wh"], wh_loads)

        @block.sync
        def _(sp):
            for k in range(wh_there, NC):
                v = wh[k * P:(k + 1) * P, :]
                sp.dma_start(stage[:, k, 0:D], v[:, 3 * D:]).then_inc(s["wh"], 16)
                sp.dma_start(stage[:, k, D:], v[:, 0:3 * D]).then_inc(s["wh"], 16)
            with nc.allow_non_contiguous_dma(reason="the bias of a column tile's units, on each of its rows"):
                for j in range(NJ):
                    v = b.rearrange("(o gc j i) -> j o gc i", o=1, j=NJ, i=Q)[j]
                    rows = bias[Q * j:Q * (j + 1), :].rearrange("p (gc i) -> p gc i", i=Q)
                    sp.dma_start(rows[:, 0:NC, :], v[:, 3 * NC:, :].broadcast_to([Q, NC, Q])).then_inc(s["bias"], 16)
                    sp.dma_start(rows[:, NC:, :], v[:, 0:3 * NC, :].broadcast_to([Q, 3 * NC, Q])).then_inc(s["bias"], 16)
            for dst, src in also_load:
                sp.dma_start(dst, src).then_inc(s["next"], 16)
            if also_load:
                sp.wait_ge(s["next"], 16 * len(also_load))

        @block.gpsimd
        def _(pool):
            nc.gpsimd.memset(HH[:], 0.0).then_inc(s["xadd"], 1)
            nc.gpsimd.tensor_copy(XC[:], xt[:, :, 0:UB]).then_inc(s["xc"], 1)
            nc.gpsimd.memset(SEL[:], 0.0).then_inc(s["sel0"], 1)
            pool.wait_ge(s["sel0"], 1)
            nc.gpsimd.affine_select(out=SEL[:, :, :, 0:B], in_=SEL[:, :, :, 0:B], compare_op=ALU.not_equal, fill=1.0, base=0,
                                    pattern=[[-B, U], [-Q, NJ], [-1, B]], channel_multiplier=1).then_inc(s["sel1"], 1)
            pool.wait_ge(s["amax"], 1)
            nc.gpsimd.partition_all_reduce(amaxall[:], amax[:], P, bass.bass_isa.ReduceOp.max).then_inc(s["amaxall"], 1)
            with pool.Fori(0, rounds) as r:
                pool.wait_ge(s["xw"], r + 1)
                nc.gpsimd.tensor_copy(XC[:], xt[:, :, bass.ds((r + 1) * UB, UB)]).then_inc(s["xc"], 1)
                pool.wait_ge(s["h"], r * U + (U + 1))
                for c in range(NC):
                    here = xt[:, c, bass.ds(r * UB, UB)].rearrange("p (u b) -> p u b", b=B)
                    last = nc.gpsimd.tensor_tensor(here, here, HH[:].rearrange("p u (c b) -> p u c b", b=B)[:, :, c, :], ALU.add)
                last.then_inc(s["xadd"], 1)

        @block.tensor
        def _(pe):
            def x_product(n):
                k, half = divmod(n, 2)
                lo, hi = half * (NG // 2), (half + 1) * (NG // 2)
                for j in range(NJ):
                    last = nc.tensor.matmul(PX[Q * j:Q * j + UB, lo * Q:hi * Q], XC[:, k, :], tile_cols(wx_sb, k, j, lo, hi),
                                            start=(n == 0), stop=(n == U - 1), skip_group_check=True)
                return last

            def seed(u, bank, lo, hi):
                for j in range(NJ):
                    last = nc.tensor.matmul(bank[Q * j:Q * j + 2 * B, 0:(hi - lo) * Q], SEL[:, u, j, :], XR[:, lo * Q:hi * Q],
                                            start=True, stop=False, skip_group_check=True)
                return last

            pe.wait_ge(s["xc"], 1)
            for n in range(U):
                last = x_product(n)
            wh_arrived(pe)
            for k in range(NC):
                for j in range(NJ):
                    last = nc.tensor.matmul(PX[Q * j:Q * j + B, :], m.cond[:, k, :], tile_cols(stage, k, j, 0, NG),
                                            start=False, stop=True, skip_group_check=True)
            last.then_inc(s["xw"], 1)
            pe.wait_ge(s["zero"], 1)
            pe.wait_ge(s["lo"], NC * NJ)
            pe.wait_ge(s["hi"], NC)
            pe.wait_ge(s["sel"], 1)
            pe.wait_ge(s["xr"], 1)
            seed(0, PG, 0, 3 * NC)
            seed(0, PO, 3 * NC, NG)
            with pe.Fori(0, rounds) as r:
                for u in range(U):
                    now = pe.snap(r * U + (u + 1))
                    pe.wait_ge(s["h"], now)
                    for bank, lo, hi, done in ((PG, 0, 3 * D // NJ, "gif"), (PO, 3 * D // NJ, D, "o")):
                        for k in range(NC):
                            for part in range(2):
                                for j in range(NJ):
                                    last = nc.tensor.matmul(bank[Q * j:Q * j + 2 * B, 0:hi - lo], H[:, u % 2, k, :],
                                                            w16[:, part, k, j, lo:hi], start=False,
                                                            stop=(k == NC - 1 and part == 1), skip_group_check=True)
                        last.then_inc(s[done], 1)
                    if u == 0:
                        pe.wait_ge(s["xc"], r + 2)
                    if u < U - 1:
                        x_product(u)
                    if u == U - 2:
                        x_product(U - 1)
                    if u == U - 1:
                        pe.wait_ge(s["xr"], r + 2)
                    pe.wait_ge(s["trg"], now)
                    seed((u + 1) % U, PG, 0, 3 * NC)
                    pe.wait_ge(s["tro"], now)
                    last = seed((u + 1) % U, PO, 3 * NC, NG)
                    if u == U - 2:
                        last.then_inc(s["xw"], 1)

        @block.scalar
        def _(act):
            wh_arrived(act)
            act.wait_ge(s["sc"], 1)
            for k in range(NC):
                for j in range(NJ):
                    last = nc.scalar.activation(w16[:, 0, k, j, :].rearrange("p (gc i) -> p gc i", i=Q),
                                                tile_cols(stage, k, j, 0, NG), ACT.Copy, scale=sc[:])
                last.then_inc(s["hi"], 1)
            def steps(scale):
                nc.scalar.activation(one_sig[:], m.eps[:], ACT.Sigmoid)
                with act.Fori(0, rounds) as r:
                    for u in range(U):
                        now = act.snap(r * U + (u + 1))
                        act.wait_ge(s["preg"], now)
                        nc.scalar.activation(G, PREG, ACT.Tanh, scale=scale)
                        act.wait_ge(s["pre"], now)
                        nc.scalar.activation(SIF[:].rearrange("p g n -> p (g n)"), PRE, ACT.Sigmoid, scale=scale).then_inc(s["ifd"], 1)
                        act.wait_ge(s["preo"], now)
                        nc.scalar.activation(SO[:], PREO, ACT.Sigmoid, scale=scale)
                        act.wait_ge(s["c"], now)
                        nc.scalar.activation(TC, C, ACT.Tanh).then_inc(s["tc"], 1)

            act.wait_ge(s["usual"], 1)
            usual = act.value_load(usual_i[0:1, 0:1], min_val=0, max_val=1)
            with act.If(usual != 0):
                steps(1.0 / (W_TOP * H_SCALE))
            with act.Else():
                steps(inv[:])

        @block.vector
        def _(dve):
            for bank in (PG, PO):
                last = nc.vector.memset(bank[:], 0.0)
            nc.vector.memset(C, 0.0).then_inc(s["zero"], 1)
            wh_arrived(dve)
            nc.vector.tensor_reduce(amax[:], stage, AX.XY, ALU.max, apply_absolute_value=True).then_inc(s["amax"], 1)
            dve.wait_ge(s["amaxall"], 1)
            nc.vector.tensor_scalar(e2[:].bitcast(I32), amaxall[:].bitcast(I32), 0x7F800000, None, ALU.bitwise_and).then_inc(s["e2"], 1)
            dve.wait_ge(s["e2"], 1)
            nc.vector.tensor_scalar(e2[:], e2[:], 2.0 ** -80, 2.0 ** 80, ALU.max, ALU.min).then_inc(s["e2c"], 1)
            dve.wait_ge(s["e2c"], 1)
            nc.vector.tensor_scalar(low[:], e2[:], USUAL[0], None, ALU.is_ge).then_inc(s["us"], 1)
            dve.wait_ge(s["us"], 1)
            nc.vector.scalar_tensor_tensor(low[:], e2[:], USUAL[1], low[:], ALU.is_le, ALU.mult).then_inc(s["us"], 1)
            nc.vector.tensor_scalar(one_less[:], e2[:], -1.0, 1.0, ALU.mult, ALU.add).then_inc(s["us"], 1)
            dve.wait_ge(s["us"], 3)
            nc.vector.tensor_copy(usual_i[:], low[:]).then_inc(s["usual"], 1)
            nc.vector.scalar_tensor_tensor(e2[:], one_less[:], low[:], e2[:], ALU.mult, ALU.add).then_inc(s["us"], 1)
            dve.wait_ge(s["us"], 4)
            nc.vector.reciprocal(rcp[:], e2[:]).then_inc(s["rcp"], 1)
            dve.wait_ge(s["rcp"], 1)
            nc.vector.tensor_scalar(sc[:], rcp[:], W_TOP, None, ALU.mult).then_inc(s["sc"], 1)
            nc.vector.tensor_scalar(inv[:], e2[:], 1.0 / (W_TOP * H_SCALE), None, ALU.mult).then_inc(s["rcp"], 1)
            dve.wait_ge(s["sc"], 1)
            nc.vector.tensor_scalar(outv[:], sc[:], H_SCALE, None, ALU.mult).then_inc(s["rcp"], 1)
            dve.wait_ge(s["rcp"], 3)
            dve.wait_ge(s["sel1"], 1)
            nc.vector.tensor_scalar(SEL[:].rearrange("p u j m -> p (u j m)"), SEL[:].rearrange("p u j m -> p (u j m)"), outv[:], None,
                                    ALU.mult).then_inc(s["sel"], 1)
            for k in range(NC):
                dve.wait_ge(s["hi"], k + 1)
                for j in range(NJ):
                    view = lambda part: w16[:, part, k, j, :].rearrange("p (gc i) -> p gc i", i=Q)
                    nc.vector.scalar_tensor_tensor(view(1), tile_cols(stage, k, j, 0, NG), sc[:], view(0),
                                                   ALU.mult, ALU.subtract).then_inc(s["lo"], 1)
            dve.wait_ge(s["zero"], 1)
            dve.wait_ge(s["rcp"], 3)
            nc.vector.memset(H[:], 0.0).then_inc(s["h"], 1)
            dve.wait_ge(s["bias"], 16 * 2 * NJ)
            dve.wait_ge(s["xw"], 1)
            nc.vector.tensor_tensor(XR[:], PX[:], bias[:], ALU.add).then_inc(s["xr"], 1)
            with dve.Fori(0, rounds) as r:
                for u in range(U):
                    now = dve.snap(r * U + (u + 1))
                    if u == U - 1:
                        dve.wait_ge(s["xw"], r + 2)
                        nc.vector.tensor_tensor(XR[:], PX[:], bias[:], ALU.add).then_inc(s["xr"], 1)

                    dve.wait_ge(s["gif"], now)
                    nc.vector.transpose(GT[:, 0:NC, :].rearrange("p g n -> p (g n)"), PG[:, 0:NC * Q]).then_inc(s["trg0"], 1)
                    nc.vector.transpose(GT[:, NC:, :].rearrange("p g n -> p (g n)"), PG[:, NC * Q:3 * NC * Q]).then_inc(s["trg"], 1)
                    dve.wait_ge(s["trg0"], now)
                    nc.vector.tensor_tensor(by_unit(PREG), GT[:, 0:NC, 0:B], GT[:, 0:NC, B:2 * B], ALU.add).then_inc(s["preg"], 1)
                    dve.wait_ge(s["trg"], now)
                    nc.vector.tensor_tensor(by_unit(PRE), GT[:, NC:, 0:B], GT[:, NC:, B:2 * B],
                                            ALU.add).then_inc(s["pre"], 1)
                    dve.wait_ge(s["o"], now)
                    nc.vector.transpose(OT[:].rearrange("p g n -> p (g n)"), PO[:, 0:NC * Q]).then_inc(s["tro"], 1)
                    dve.wait_ge(s["ifd"], now)
                    nc.vector.tensor_tensor(IGFC[:].rearrange("p g n -> p (g n)"), SIF[:].rearrange("p g n -> p (g n)"), GC,
                                            ALU.mult).then_inc(s["ig"], 1)
                    dve.wait_ge(s["tro"], now)
                    nc.vector.tensor_tensor(by_unit(PREO), OT[:, :, 0:B], OT[:, :, B:2 * B], ALU.add).then_inc(s["preo"], 1)
                    dve.wait_ge(s["ig"], now)
                    nc.vector.tensor_tensor(C, IGFC[:, 0, :], IGFC[:, 1, :], ALU.add).then_inc(s["c"], 1)
                    dve.wait_ge(s["tc"], now)
                    if u == 0:
                        dve.wait_ge(s["xadd"], r + 1)
                    nxt = H[:, (u + 1) % 2]
                    nc.vector.tensor_tensor(HH[:, u, :], SO[:], TC, ALU.mult)
                    nc.vector.scalar_tensor_tensor(nxt[:, :, 0:B], by_unit(SO[:]), H_SCALE, by_unit(TC), ALU.mult, ALU.mult).then_inc(s["hhi"], 1)
                    dve.wait_ge(s["hhi"], now)
                    nc.vector.scalar_tensor_tensor(nxt[:, :, B:2 * B], by_unit(HH[:, u, :]), H_SCALE, nxt[:, :, 0:B],
                                                   ALU.mult, ALU.subtract).then_inc(s["h"], 1)
            dve.wait_ge(s["xadd"], rounds + 1)


def gated_scan(nc, m, biases2, pad, weights, wx, wh, ahead):
    with ExitStack() as ctx:
        s = Sems(nc, ctx, "g_", "next tw cw z f i gs rg fn inm ni ln one lc ex0 ex1 sn hid sum out small")
        sbt = lambda n, shape, dt=F32: ctx.enter_context(nc.sbuf_tensor("g_" + n, shape, dt))
        banks = [ctx.enter_context(nc.psum_tensor(f"g_z{i}", [P, 512], F32)) for i in range(8)]
        TBB = P * B
        natural = m.natural_weights()
        wt = m.scratch[:, 0:3 * NC * D].rearrange("p (w k h) -> p w k h", w=3, k=NC)
        F = sbt("F", [P, 2, TBB])
        I = sbt("I", [P, 2, TBB])
        GS = sbt("GS", [P, TBB])
        LC = sbt("LC", [P, 2, T + 1])
        ni_buf = [m.scratch[:, 3 * NC * D + i * XCOLS:3 * NC * D + (i + 1) * XCOLS] for i in range(2)]
        items = [(c, n) for c in range(NC + 1) for n in range(TB)]
        block = ctx.enter_context(nc.Block())
        row = lambda a, b: a.rearrange("p (t b) -> p b t", b=B)[:, b, :]
        lr = lambda c: m.xb[:, c, 0:XCOLS]

        def blocks_and_scans(on_block, on_first, on_second):
            for c, n in items:
                if c < NC:
                    on_block(c, n, c * TB + n)
                if c > 0:
                    q = (c - 1) * B + n // 2
                    (on_second if n % 2 else on_first)(c - 1, n // 2, q)

        @block.sync
        def _(sp):
            with nc.allow_non_contiguous_dma(reason="small vectors, features to partitions"):
                for dst, src in biases2:
                    sp.dma_start(dst, src).then_inc(s["small"], 16)
            sp.wait_ge(s["small"], 16 * len(biases2))
            sp.wait_ge(s["z"], 3 * NC * TB)
            sp.wait_ge(s["out"], (NC - 1) * B)
            gates_first(weights[0], wx, sp, s["next"])
            gates_first(weights[1], wh, sp, s["next"], range(ahead))
            sp.wait_ge(s["next"], 64)

        @block.gpsimd
        def _(pool):
            nc.gpsimd.memset(pad, 0.0)
            for q in range(NC * B):
                c, b = divmod(q, B)
                pool.wait_ge(s["sum"], q + 1)
                nc.gpsimd.tensor_tensor(row(lr(c), b), row(lr(c), b), row(m.xa[:, c, 0:XCOLS], b), ALU.add).then_inc(s["out"], 1)

        @block.tensor
        def _(pe):
            for n in range(3 * NC):
                w, k = divmod(n, NC)
                if n >= 8:
                    pe.wait_ge(s["cw"], n - 7)
                for h in range(NC):
                    last = nc.tensor.transpose(banks[n % 8][:, h * P:(h + 1) * P], natural[:, w * NC + h, k * P:(k + 1) * P], m.ident[:])
                last.then_inc(s["tw"], 1)
            pe.wait_ge(s["cw"], 3 * NC)
            for n in range(NC * TB):
                c, blk = divmod(n, TB)
                if n >= 2:
                    pe.wait_ge(s["f"], n - 1)
                    pe.wait_ge(s["i"], n - 1)
                    pe.wait_ge(s["ni"], n - 1)
                for w in range(3):
                    for k in range(NC):
                        last = nc.tensor.matmul(banks[w * 2 + n % 2][:], wt[:, w, k, c * P:(c + 1) * P],
                                                m.xa[:, k, blk * TBB:(blk + 1) * TBB], start=(k == 0), stop=(k == NC - 1))
                    last.then_inc(s["z"], 1)

        @block.scalar
        def _(act):
            act.wait_ge(s["small"], 16 * len(biases2))

            def gates(c, blk, n):
                act.wait_ge(s["z"], 3 * n + 1)
                if n >= 2:
                    act.wait_ge(s["ni"], n - 1)
                nc.scalar.activation(F[:, n % 2], banks[n % 2][:], ACT.Sigmoid, bias=m.bias2[:, 0, c:c + 1]).then_inc(s["f"], 1)
                act.wait_ge(s["z"], 3 * n + 2)
                nc.scalar.activation(I[:, n % 2], banks[2 + n % 2][:], ACT.Sigmoid, bias=m.bias2[:, 1, c:c + 1]).then_inc(s["i"], 1)
                act.wait_ge(s["fn"], n + 1)
                nc.scalar.activation(lr(c)[:, blk * TBB:(blk + 1) * TBB], F[:, n % 2], ACT.Ln, bias=m.eps[:]).then_inc(s["ln"], 1)

            def exponentials(c, b, q):
                act.wait_ge(s["lc"], q + 1)
                lc = LC[:, q % 2]
                nc.scalar.activation(row(lr(c), b), lc[:, 0:T], ACT.Exp, scale=-1.0, bias=lc[:, T:T + 1]).then_inc(s["ex0"], 1)
                act.wait_ge(s["ex0"], q + 1)
                nc.scalar.activation(lc[:, 1:T + 1], lc[:, 1:T + 1], ACT.Exp).then_inc(s["ex1"], 1)

            blocks_and_scans(gates, exponentials, lambda c, b, q: None)

        @block.vector
        def _(dve):
            nc.vector.memset(LC[:, :, 0:1], 0.0).then_inc(s["one"], 1)
            for n in range(3 * NC):
                w, k = divmod(n, NC)
                dve.wait_ge(s["tw"], n + 1)
                nc.vector.tensor_copy(wt[:, w, k, :], banks[n % 8][:]).then_inc(s["cw"], 1)
            dve.wait_ge(s["one"], 1)
            dve.wait_ge(s["small"], 16 * len(biases2))
            running = m.one[:].broadcast_to([P, T])

            def ratios(c, blk, n):
                f, i = F[:, n % 2], I[:, n % 2]
                dve.wait_ge(s["f"], n + 1)
                dve.wait_ge(s["i"], n + 1)
                nc.vector.scalar_tensor_tensor(GS[:], f, 1e-8, i, ALU.add, ALU.add).then_inc(s["gs"], 1)
                dve.wait_ge(s["gs"], n + 1)
                nc.vector.reciprocal(GS[:], GS[:]).then_inc(s["rg"], 1)
                dve.wait_ge(s["rg"], n + 1)
                nc.vector.tensor_tensor(f, f, GS[:], ALU.mult).then_inc(s["fn"], 1)
                nc.vector.tensor_tensor(i, i, GS[:], ALU.mult).then_inc(s["inm"], 1)
                dve.wait_ge(s["inm"], n + 1)
                dve.wait_ge(s["z"], 3 * n + 3)
                if blk == 0 and c >= 2:
                    dve.wait_ge(s["hid"], (c - 1) * B)
                nc.vector.scalar_tensor_tensor(ni_buf[c % 2][:, blk * TBB:(blk + 1) * TBB], banks[4 + n % 2][:],
                                               m.bias2[:, 2, c:c + 1], i, ALU.add, ALU.mult).then_inc(s["ni"], 1)

            def log_scan(c, b, q):
                dve.wait_ge(s["ln"], (c + 1) * TB)
                if q >= 2:
                    dve.wait_ge(s["sum"], q - 1)
                nc.vector.tensor_tensor_scan(LC[:, q % 2, 1:T + 1], running, row(lr(c), b), 0.0, ALU.mult, ALU.add).then_inc(s["lc"], 1)

            def hidden_scan(c, b, q):
                ni = row(ni_buf[c % 2], b)
                dve.wait_ge(s["ni"], (c + 1) * TB)
                dve.wait_ge(s["ex0"], q + 1)
                nc.vector.tensor_tensor(ni, ni, row(lr(c), b), ALU.mult).then_inc(s["sn"], 1)
                dve.wait_ge(s["sn"], q + 1)
                nc.vector.tensor_tensor_scan(row(lr(c), b), running, ni, 0.0, ALU.mult, ALU.add).then_inc(s["hid"], 1)
                dve.wait_ge(s["hid"], q + 1)
                dve.wait_ge(s["ex1"], q + 1)
                nc.vector.scalar_tensor_tensor(row(lr(c), b), LC[:, q % 2, 1:T + 1], m.cond[:, c, b:b + 1], row(lr(c), b),
                                               ALU.mult, ALU.add).then_inc(s["sum"], 1)

            blocks_and_scans(ratios, log_scan, hidden_scan)


def store(nc, m, out):
    with ExitStack() as ctx:
        s = Sems(nc, ctx, "s_", "tp cpv cps out")
        tp = [ctx.enter_context(nc.psum_tensor(f"s_tp{i}", [P, 512], F32)) for i in range(8)]
        xo = m.xa_all[:, 0:B * TB * D].rearrange("p (n d) -> p n d", d=D)
        block = ctx.enter_context(nc.Block())

        @block.tensor
        def _(pe):
            for n in range(B * TB):
                b, tb = divmod(n, TB)
                if n >= 8:
                    pe.wait_ge(s["cpv"] if n % 2 == 0 else s["cps"], (n - 8) // 2 + 1)
                for c in range(NC):
                    src = m.xb[:, c, 0:XCOLS].rearrange("p (t b) -> p b t", b=B)[:, b, tb * P:(tb + 1) * P]
                    last = nc.tensor.transpose(tp[n % 8][:, c * P:(c + 1) * P], src, m.ident[:])
                last.then_inc(s["tp"], 1)

        @block.vector
        def _(dve):
            for n in range(0, B * TB, 2):
                dve.wait_ge(s["tp"], n + 1)
                nc.vector.tensor_copy(xo[:, n, :], tp[n % 8][:]).then_inc(s["cpv"], 1)

        @block.scalar
        def _(act):
            for n in range(1, B * TB, 2):
                act.wait_ge(s["tp"], n + 1)
                nc.scalar.activation(xo[:, n, :], tp[n % 8][:], ACT.Copy).then_inc(s["cps"], 1)

        @block.sync
        def _(sp):
            for n in range(0, B * TB, 2):
                b, tb = divmod(n, TB)
                sp.wait_ge(s["cpv"], n // 2 + 1)
                sp.wait_ge(s["cps"], n // 2 + 1)
                sp.dma_start(out[b, tb * P:(tb + 2) * P, :].rearrange("(n p) d -> p n d", p=P), xo[:, n:n + 2, :]).then_inc(s["out"], 16)
            sp.wait_ge(s["out"], 16 * (B * TB // 2))


class Memory:

    def __init__(self, nc, ctx):
        sbt = lambda n, shape: ctx.enter_context(nc.sbuf_tensor(n, shape, F32))
        self.xa_all = sbt("xa", [P, NC * XPAD])
        self.xb_all = sbt("xb", [P, NC * XPAD])
        self.scratch = sbt("scratch", [P, 14 * T])
        self.xa = self.xa_all[:].rearrange("p (c n) -> p c n", c=NC)
        self.xb = self.xb_all[:].rearrange("p (c n) -> p c n", c=NC)
        self.ident = sbt("ident", [P, P])
        self.cond = sbt("cond", [P, NC, B])
        self.bias2 = sbt("bias2", [P, 3, NC])
        self.eps = sbt("eps", [P, 1])
        self.one = sbt("one", [P, 1])
        self.small = sbt("small", [P, 7 * B * NC])

    def natural_weights(self):
        return self.scratch[:, NC * G4:NC * G4 + 3 * NC * D].rearrange("p (n d) -> p n d", d=D)

    def lstm_weights(self, region):
        half = NC * G4
        fp32 = [region[:, i * half:(i + 1) * half].rearrange("p (k n) -> p k n", k=NC) for i in range(2)]
        parts = self.scratch[:, 0:half].bitcast(F16).rearrange("p (s k j n) -> p s k j n", s=2, k=NC, j=NJ)
        return fp32 + [parts]


def program(nc, x, cond, wx1, wh1, b1, wf, bf, wi, bi, wh, bh, wx3, wh3, b3, out):
    with ExitStack() as ctx:
        m = Memory(nc, ctx)

        units = lambda b: b.rearrange("(c p) -> p c", p=P)
        weights1, weights3 = m.lstm_weights(m.xb_all), m.lstm_weights(m.xa_all)
        ahead = ((NC - 1) * XPAD - NC * G4) // G4
        natural = m.natural_weights()
        load_and_sparsify(nc, m, x, cond, [(weights1[0], wx1), (weights1[1], wh1)])
        lstm(nc, m, "p_", m.xa, weights1, wh1, b1, NC,
             also_load=[(natural[:, w * NC:(w + 1) * NC, :], a.rearrange("(h p) d -> p h d", p=P)) for w, a in enumerate((wf, wi, wh))])
        gated_scan(nc, m, [(m.bias2[:, w, :], units(b)) for w, b in enumerate((bf, bi, bh))], m.xb[:, :, XCOLS:XPAD],
                   weights3, wx3, wh3, ahead)
        lstm(nc, m, "q_", m.xb, weights3, wh3, b3, ahead)
        store(nc, m, out)


_INS = ['x', 'cond_1024', 'L1_cond_Wx', 'L1_cond_Wh', 'L1_cond_b', 'L2_cond_W_f', 'L2_cond_b_f', 'L2_cond_W_i',
        'L2_cond_b_i', 'L2_cond_W_h', 'L2_cond_b_h', 'L3_cond_Wx', 'L3_cond_Wh', 'L3_cond_b']


def kernel(**inputs):
    import numpy as _np
    import concourse.bacc as _bacc
    from concourse import mybir as _mybir
    from concourse.bass_utils import run_bass_kernel_spmd as _run

    nc = _bacc.Bacc("TRN2", target_bir_lowering=False, num_devices=1)
    arrays, args = {}, []
    for name in _INS:
        a = _np.ascontiguousarray(inputs[name])
        arrays[f"in_{name}_dram"] = a
        args.append(nc.dram_tensor(f"in_{name}_dram", a.shape, _mybir.dt.from_np(a.dtype), kind="ExternalInput").ap())
    args.append(nc.dram_tensor("out_0_dram", (B, T, D), _mybir.dt.float32, kind="ExternalOutput").ap())
    program(nc, *args)
    r = _run(nc, [arrays], core_ids=[0])
    return r.results[0]["out_0_dram"]
```

```python
import concourse.bass as bass
from concourse import mybir
from contextlib import ExitStack


F32 = mybir.dt.float32
F16 = mybir.dt.float16
BF16 = mybir.dt.bfloat16
I32 = mybir.dt.int32
ALU = mybir.AluOpType
ACT = mybir.ActivationFunctionType
AX = mybir.AxisListType

B, T, D = 4, 1024, 512
P = 128
NC = D // P
Q = 32
NJ = P // Q
G4 = 4 * D
NG = 4 * NC
TB = T // P
U = 8
UB = U * B
ROUNDS = T // U
XCOLS = T * B
EARLY = 3
XTAIL = 2 * UB
NF = NC // 2
RUNS = ((0, 3, 1), (0, 0, 3), (NF, 3, 1), (NF, 0, 3))
GA = NG // 2
USUAL = (2.0 ** -6, 1.0)
H_SCALE = 2.0 ** 12
W_TOP = 2.0 ** 14
BIG = 3.0e38


class Sems:

    def __init__(self, nc, ctx, prefix, names):
        self.h = {n: ctx.enter_context(nc.semaphore(prefix + n)) for n in names.split()}

    def __getitem__(self, n):
        return self.h[n]


def in_chip_order():
    at = 0
    for chunk, gate, n in RUNS:
        yield at, slice(gate, gate + n), slice(chunk, chunk + NF)
        at += n * NF


def load_weight(dst, src, sp, sem, chunks=range(NC)):
    v = src.rearrange("(k p) (g m) -> p k g m", p=P, g=4)
    for k in chunks:
        for at, gates, units in in_chip_order():
            n = (gates.stop - gates.start) * NF
            sp.dma_start(dst[:, k, at * P:(at + n) * P].rearrange("p (g m) -> p g m", m=NF * P),
                         v[:, k, gates, units.start * P:units.stop * P]).then_inc(sem, 16)


def load_and_sparsify(nc, m, x, cond, lstm_loads):
    with ExitStack() as ctx:
        s = Sems(nc, ctx, "a_", "x0 x1 cond weights id0 tp cpv cps one absd recs recl expd thd zs cum le "
                                "hot gat gate2 msk upd recp")
        tp = [ctx.enter_context(nc.psum_tensor(f"tp{i}", [P, 512], F32)) for i in range(8)]
        PART = 4
        ring = m.scratch[:, 0:2 * PART * D].rearrange("p (n d) -> p n d", d=D)
        w = [m.scratch[:, 2 * PART * D + i * T:2 * PART * D + (i + 1) * T] for i in range(8)]
        ax, pi, dd = w[0:4], w[4:6], w[6:8]
        gm = ctx.enter_context(nc.sbuf_tensor("gm", [P, 2, T], F32))
        mk = ctx.enter_context(nc.sbuf_tensor("mk", [P, 2, T + 1], F32))
        sm = m.small
        n_tiles = B * NC
        block = ctx.enter_context(nc.Block())

        def col(k, n):
            return sm[:, k * n_tiles + n:k * n_tiles + n + 1]

        def xt(n):
            b, c = divmod(n, NC)
            return m.xa[:, c, 0:XCOLS].rearrange("p (t b) -> p b t", b=B)[:, b, :]

        @block.sync
        def _(sp):
            for k in range(B * TB // PART):
                if k >= 2:
                    sp.wait_ge(s["tp"], PART * (k - 1))
                b, half = divmod(k, TB // PART)
                sp.dma_start(ring[:, (k % 2) * PART:(k % 2 + 1) * PART, :],
                             x[b, half * PART * P:(half + 1) * PART * P, :].rearrange("(n p) d -> p n d", p=P)).then_inc(s[f"x{k % 2}"], 16)
                if k == 1:
                    with nc.allow_non_contiguous_dma(reason="small vectors, features to partitions"):
                        for c in range(NC):
                            sp.dma_start(m.cond[:, c, :], cond[:, c * P:(c + 1) * P].rearrange("b p -> p b")).then_inc(s["cond"], 16)
            for dst, src in lstm_loads:
                load_weight(dst, src, sp, s["weights"])
            sp.wait_ge(s["weights"], 16 * len(RUNS) * NC * len(lstm_loads))

        @block.gpsimd
        def _(pool):
            nc.gpsimd.memset(m.ident[:], 0.0).then_inc(s["id0"], 1)
            pool.wait_ge(s["id0"], 1)
            nc.gpsimd.affine_select(out=m.ident[:], in_=m.ident[:], compare_op=ALU.not_equal, fill=1.0,
                                    base=0, pattern=[[-1, P]], channel_multiplier=1).then_inc(s["id0"], 1)
            nc.gpsimd.memset(m.eps[:], 1e-8)
            nc.gpsimd.memset(m.xa_all[:, NC * XCOLS:], 0.0).then_inc(s["one"], 1)
            for i in range(2, n_tiles + 3):
                if i - 2 < n_tiles:
                    n = i - 2
                    pool.wait_ge(s["le"], n + 1)
                    if n >= 2:
                        pool.wait_ge(s["gat"], n - 1)
                    nc.gpsimd.tensor_tensor(dd[n % 2], mk[:, n % 2, 0:T], mk[:, n % 2, 1:T + 1], ALU.subtract).then_inc(s["hot"], 1)
                if i >= 3:
                    n = i - 3
                    pool.wait_ge(s["msk"], n + 1)
                    nc.gpsimd.tensor_tensor(xt(n), xt(n), gm[:, n % 2, :], ALU.mult).then_inc(s["upd"], 1)

        @block.tensor
        def _(pe):
            pe.wait_ge(s["id0"], 2)
            for n in range(B * TB):
                if n % PART == 0:
                    k = n // PART
                    pe.wait_ge(s[f"x{k % 2}"], 16 * (k // 2 + 1))
                if n >= 8:
                    pe.wait_ge(s["cpv"] if n % 2 == 0 else s["cps"], (n - 8) // 2 + 1)
                for c in range(NC):
                    last = nc.tensor.transpose(tp[n % 8][:, c * P:(c + 1) * P], ring[:, n % (2 * PART), c * P:(c + 1) * P], m.ident[:])
                last.then_inc(s["tp"], 1)

        def out_of(n):
            b, tb = divmod(n, TB)
            dst = m.xa[:, :, 0:XCOLS].rearrange("p c (t b) -> p c b t", b=B)[:, :, b, tb * P:(tb + 1) * P]
            return dst, tp[n % 8][:].rearrange("p (c t) -> p c t", c=NC)

        @block.scalar
        def _(act):
            def absolute(n):
                if n % NC == 0:
                    act.wait_ge(s["cpv"], (n // NC + 1) * TB // 2)
                    act.wait_ge(s["cps"], (n // NC + 1) * TB // 2)
                if n >= 4:
                    act.wait_ge(s["msk"], n - 3)
                nc.scalar.activation(ax[n % 4], xt(n), ACT.Abs, accum_out=col(0, n)).then_inc(s["absd"], 1)

            def exponential(n):
                act.wait_ge(s["recs"], n + 1)
                if n >= 2:
                    act.wait_ge(s["le"], n - 1)
                nc.scalar.activation(pi[n % 2], ax[n % 4], ACT.Exp, scale=col(2, n), accum_out=col(3, n)).then_inc(s["expd"], 1)

            def thresholds(n):
                act.wait_ge(s["recp"], n + 1)
                nc.scalar.activation(pi[n % 2], pi[n % 2], ACT.Copy, scale=col(4, n)).then_inc(s["thd"], 1)

            for i in range(n_tiles + 2):
                b, c = divmod(i, NC)
                if c == 0 and b < B:
                    for n in range(b * TB + 1, (b + 1) * TB, 2):
                        act.wait_ge(s["tp"], n + 1)
                        dst, src = out_of(n)
                        nc.scalar.activation(dst, src, ACT.Copy).then_inc(s["cps"], 1)
                if i >= 2:
                    thresholds(i - 2)
                if i < n_tiles:
                    absolute(i)
                if 1 <= i <= n_tiles:
                    exponential(i - 1)

        @block.vector
        def _(dve):
            nc.vector.memset(m.one[:], 1.0).then_inc(s["zs"], 1)
            nc.vector.memset(mk[:, :, 0:1], 1.0).then_inc(s["zs"], 1)
            dve.wait_ge(s["zs"], 2)
            running = m.one[:].broadcast_to([P, T])

            def reciprocal(n):
                dve.wait_ge(s["absd"], n + 1)
                nc.vector.reciprocal(col(1, n), col(0, n)).then_inc(s["recl"], 1)
                dve.wait_ge(s["recl"], n + 1)
                nc.vector.tensor_scalar(col(2, n), col(1, n), 2.0, None, ALU.mult).then_inc(s["recs"], 1)

            def reciprocal_pi(n):
                dve.wait_ge(s["expd"], n + 1)
                nc.vector.reciprocal(col(4, n), col(3, n)).then_inc(s["recp"], 1)

            def cumulate(n):
                b, c = divmod(n, NC)
                dve.wait_ge(s["thd"], n + 1)
                nc.vector.tensor_tensor_scan(pi[n % 2], running, pi[n % 2], 0.0, ALU.mult, ALU.add).then_inc(s["cum"], 1)
                dve.wait_ge(s["cum"], n + 1)
                if n >= 2:
                    dve.wait_ge(s["hot"], n - 1)
                nc.vector.tensor_scalar(mk[:, n % 2, 1:T + 1], pi[n % 2], 0.001, m.cond[:, c, b:b + 1], ALU.add, ALU.is_le).then_inc(s["le"], 1)

            def mask(n):
                dve.wait_ge(s["hot"], n + 1)
                nc.vector.tensor_tensor_reduce(out=dd[n % 2], in0=dd[n % 2], in1=ax[n % 4], scale=1.0, scalar=0.0, op0=ALU.mult,
                                               op1=ALU.add, accum_out=col(5, n)).then_inc(s["gat"], 1)
                dve.wait_ge(s["gat"], n + 1)
                nc.vector.scalar_tensor_tensor(col(6, n), mk[:, n % 2, T:T + 1], BIG, col(5, n), ALU.mult, ALU.add).then_inc(s["gate2"], 1)
                dve.wait_ge(s["gate2"], n + 1)
                if n >= 2:
                    dve.wait_ge(s["upd"], n - 1)
                nc.vector.tensor_scalar(gm[:, n % 2, :], ax[n % 4], col(6, n), 1.0, ALU.is_ge, ALU.add).then_inc(s["msk"], 1)

            dve.wait_ge(s["cond"], 16 * NC)
            for i in range(n_tiles + 3):
                b, c = divmod(i, NC)
                if c == 0 and b < B:
                    for n in range(b * TB, (b + 1) * TB, 2):
                        dve.wait_ge(s["tp"], n + 1)
                        dst, src = out_of(n)
                        nc.vector.tensor_copy(dst, src).then_inc(s["cpv"], 1)
                if i < n_tiles:
                    reciprocal(i)
                if 2 <= i < n_tiles + 2:
                    cumulate(i - 2)
                if 1 <= i <= n_tiles:
                    reciprocal_pi(i - 1)
                if i >= 3:
                    mask(i - 3)


def lstm(nc, m, tag, x_all, weights, wh, b, wh_there, rounds=ROUNDS, also_load=()):
    with ExitStack() as ctx:
        s = Sems(nc, ctx, tag, "bias exponent usual xr high rest mid low parts seeded sel0 sel1 sel amaxk amax amaxall rcp sc hi lo xc xw zero next "
                               "gates_a trg_a trif_a tr_a preg_a pre_a preo_a if_a ig_a c_a tc_a hi_a h_a "
                               "gates_b trif_b tr_b pre_b preo_b if_b ig_b c_b tc_b hi_b h_b xadd "
                               + " ".join(f"wh{k}" for k in range(wh_there, NC)))
        sbt = lambda n, shape, dt=F32: ctx.enter_context(nc.sbuf_tensor(tag + n, shape, dt))
        pst = lambda n: ctx.enter_context(nc.psum_tensor(tag + n, [P, 512], F32))
        H = sbt("H", [P, 2, NC, 2 * B], F16)
        HH = sbt("HH", [P, U, NC * B])
        XC = sbt("XC", [P, NC, UB])
        XR = sbt("XR", [P, NG * Q])
        bias = sbt("bias", [P, NG * Q])
        XM = sbt("XM", [P, 2, NG * Q], BF16)
        XP = sbt("XP", [P, 3, NG * Q], BF16)
        SEL = sbt("SEL", [P, U, NJ, Q], BF16)
        GT = sbt("GT", [P, NG, Q])
        one_sig = sbt("one_sig", [P, 1])
        low, one_less = sbt("low", [P, 1]), sbt("one_less", [P, 1])
        amaxk = sbt("amaxk", [P, NC])
        usual_i = sbt("usual_i", [P, 1], I32)
        outv, amax, amaxall, e2, rcp, sc, inv = (sbt(n, [P, 1]) for n in ("outv", "amax", "amaxall", "e2", "rcp", "sc", "inv"))
        PA, PB, PX = pst("PA"), pst("PB"), pst("PX")
        PREG, PRE, PREB, GC, TC = pst("PREG"), pst("PRE"), pst("PREB"), pst("GC"), pst("TC")
        wide = lambda a: a.rearrange("p g n -> p (g n)")

        class Group:

            def __init__(self, name, chunk, col, pre_g, pre_if):
                self.chunks = slice(chunk, chunk + NF)
                self.cols = slice(chunk * B, (chunk + NF) * B)
                m = NF * B
                self.pre_g, self.pre_if = pre_g[:, 0:m], pre_if[:, 0:2 * m]
                self.pre_o = sbt("PREO" + name, [P, m])
                self.g_and_c = GC[:, col:col + 2 * m]
                self.g, self.c = self.g_and_c[:, 0:m], self.g_and_c[:, m:]
                self.tanh_c = TC[:, col:col + m]
                self.ifo = sbt("IFO" + name, [P, 3 * m])
                self.i_f, self.o = self.ifo[:, 0:2 * m], self.ifo[:, 2 * m:]
                self.igfc = sbt("IGFC" + name, [P, 2 * m])

        first = Group("A", 0, 0, PREG, PRE)
        second = Group("B", NF, 4 * NF * B, PREB, PREB[:, NF * B:])
        wx_sb, stage, w16 = weights
        xt = x_all[:, 0:NC * XCOLS].rearrange("p (c n) -> p c n", c=NC)
        block = ctx.enter_context(nc.Block())
        tile_cols = lambda w, k, j, lo, hi: w[:, k, :].rearrange("p (gc j i) -> p gc j i", j=NJ, i=Q)[:, lo:hi, j, :]
        by_unit = lambda a: a.rearrange("p (c b) -> p c b", b=B)

        def wh_arrived(eng, chunks=range(NC)):
            for k in chunks:
                if k >= wh_there:
                    eng.wait_ge(s[f"wh{k}"], 16 * len(RUNS))

        @block.sync
        def _(sp):
            for k in range(wh_there, NC):
                load_weight(stage, wh, sp, s[f"wh{k}"], [k])
            with nc.allow_non_contiguous_dma(reason="the bias of a column tile's units, on each of its rows"):
                for j in range(NJ):
                    v = b.rearrange("(o g c j i) -> j o g c i", o=1, g=4, j=NJ, i=Q)[j]
                    rows = bias[Q * j:Q * (j + 1), :].rearrange("p (g c i) -> p g c i", c=NF, i=Q)
                    for at, gates, units in in_chip_order():
                        n = gates.stop - gates.start
                        for c in range(NF):
                            sp.dma_start(rows[:, at // NF:at // NF + n, c, :],
                                         v[:, gates, units.start + c, :].broadcast_to([Q, n, Q])).then_inc(s["bias"], 16)
            for dst, src in also_load:
                sp.dma_start(dst, src).then_inc(s["next"], 16)
            if also_load:
                sp.wait_ge(s["next"], 16 * len(also_load))

        @block.gpsimd
        def _(pool):
            nc.gpsimd.memset(HH[:], 0.0).then_inc(s["xadd"], 1)
            nc.gpsimd.tensor_copy(XC[:], xt[:, :, 0:UB]).then_inc(s["xc"], 1)
            nc.gpsimd.memset(SEL[:], 0.0).then_inc(s["sel0"], 1)
            pool.wait_ge(s["sel0"], 1)
            nc.gpsimd.affine_select(out=SEL[:, :, :, 0:B], in_=SEL[:, :, :, 0:B], compare_op=ALU.not_equal, fill=1.0, base=0,
                                    pattern=[[-B, U], [-Q, NJ], [-1, B]], channel_multiplier=1).then_inc(s["sel1"], 1)
            pool.wait_ge(s["amax"], 1)
            nc.gpsimd.partition_all_reduce(amaxall[:], amax[:], P, bass.bass_isa.ReduceOp.max).then_inc(s["amaxall"], 1)
            pool.wait_ge(s["xw"], 1)
            nc.gpsimd.tensor_copy(XC[:], xt[:, :, UB:2 * UB]).then_inc(s["xc"], 1)
            with pool.Fori(0, rounds) as r:
                pool.wait_ge(s["xw"], r + 2)
                for c in range(NC):
                    last = nc.gpsimd.tensor_copy(XC[:, c, :], x_all[:, bass.ds(r * UB + (c * XCOLS + 2 * UB), UB)])
                last.then_inc(s["xc"], 1)
                pool.wait_ge(s["h_a"], r * U + (U + 1))
                pool.wait_ge(s["h_b"], r * U + (U + 1))
                for c in range(NC):
                    here = xt[:, c, bass.ds(r * UB, UB)].rearrange("p (u b) -> p u b", b=B)
                    last = nc.gpsimd.tensor_tensor(here, here, HH[:].rearrange("p u (c b) -> p u c b", b=B)[:, :, c, :], ALU.add)
                last.then_inc(s["xadd"], 1)

        @block.tensor
        def _(pe):
            def x_product(n):
                k, half = divmod(n, 2)
                lo, hi = half * (NG // 2), (half + 1) * (NG // 2)
                for j in range(NJ):
                    last = nc.tensor.matmul(PX[Q * j:Q * j + UB, lo * Q:hi * Q], XC[:, k, :], tile_cols(wx_sb, k, j, lo, hi),
                                            start=(n == 0), stop=(n == U - 1), skip_group_check=True)
                return last

            def seed(u, bank, lo, hi):
                for i in range(3):
                    last = nc.tensor.matmul(bank[:, 0:(hi - lo) * Q], SEL[:, u].rearrange("p j m -> p (j m)"), XP[:, i, lo * Q:hi * Q],
                                            start=(i == 0), stop=False, skip_group_check=True)
                return last

            def h_product(u, k, part, bank, lo, hi):
                for j in range(NJ):
                    last = nc.tensor.matmul(bank[Q * j:Q * j + 2 * B, 0:(hi - lo) * Q], H[:, u % 2, k, :],
                                            w16[:, part, k, j, lo * Q:hi * Q], start=False,
                                            stop=(k == NC - 1 and part == 1), skip_group_check=True)
                return last

            pe.wait_ge(s["xc"], 1)
            for n in range(U):
                last = x_product(n)
            wh_arrived(pe)
            for k in range(NC):
                for j in range(NJ):
                    last = nc.tensor.matmul(PX[Q * j:Q * j + B, :], m.cond[:, k, :], tile_cols(stage, k, j, 0, NG),
                                            start=False, stop=True, skip_group_check=True)
            last.then_inc(s["xw"], 1)
            pe.wait_ge(s["lo"], NC * NJ)
            pe.wait_ge(s["hi"], NC)
            pe.wait_ge(s["sel"], 1)
            pe.wait_ge(s["parts"], 1)
            pe.wait_ge(s["low"], 1)
            seed(0, PA, 0, GA)
            seed(0, PB, GA, NG)
            pe.wait_ge(s["xc"], 2)
            for n in range(EARLY):
                x_product(n)
            first_half = [(k, part) for k in range(NF) for part in range(2)]
            second_half = [(k, part) for k in range(NF, NC) for part in range(2)]
            in_between = first_half[:2]
            with pe.Fori(0, rounds) as r:
                for u in range(U):
                    now = pe.snap(r * U + (u + 1))
                    pe.wait_ge(s["h_a"], now)
                    for k, part in first_half:
                        h_product(u, k, part, PA, 0, GA)
                    for k, part in in_between:
                        h_product(u, k, part, PB, GA, NG)
                    pe.wait_ge(s["h_b"], now)
                    for k, part in second_half:
                        last = h_product(u, k, part, PA, 0, GA)
                    last.then_inc(s["gates_a"], 1)
                    for k, part in first_half + second_half:
                        if (k, part) not in in_between:
                            last = h_product(u, k, part, PB, GA, NG)
                    last.then_inc(s["gates_b"], 1)
                    if u == U - 1:
                        pe.wait_ge(s["parts"], r + 2)
                        pe.wait_ge(s["low"], r + 2)
                    pe.wait_ge(s["tr_a"], now)
                    seed((u + 1) % U, PA, 0, GA)
                    if u == U - EARLY:
                        pe.wait_ge(s["xr"], r + 2)
                        pe.wait_ge(s["xc"], r + 3)
                    last = x_product((u + EARLY) % U)
                    if u == U - EARLY - 1:
                        last.then_inc(s["xw"], 1)
                    pe.wait_ge(s["tr_b"], now)
                    last = seed((u + 1) % U, PB, GA, NG)
                    if u == U - 2:
                        last.then_inc(s["seeded"], 1)

        @block.scalar
        def _(act):
            def part_of_xr(i, made, n, done):
                act.wait_ge(s[made], n)
                nc.scalar.activation(XM[:, i], XR[:], ACT.Copy).then_inc(s[done], 1)

            def publish_parts():
                nc.scalar.activation(XP[:, 0:2], XM[:], ACT.Copy).then_inc(s["parts"], 1)

            wh_arrived(act)
            act.wait_ge(s["sc"], 1)
            for k in range(NC):
                for j in range(NJ):
                    last = nc.scalar.activation(w16[:, 0, k, j, :].rearrange("p (gc i) -> p gc i", i=Q),
                                                tile_cols(stage, k, j, 0, NG), ACT.Copy, scale=sc[:])
                last.then_inc(s["hi"], 1)
                if k == 1:
                    part_of_xr(0, "xr", 1, "high")
                if k == 2:
                    part_of_xr(1, "rest", 1, "mid")
            act.wait_ge(s["mid"], 1)
            publish_parts()

            def steps(scale):
                nc.scalar.activation(one_sig[:], m.eps[:], ACT.Sigmoid)
                with act.Fori(0, rounds) as r:
                    for u in range(U):
                        now = act.snap(r * U + (u + 1))
                        if u == U - 3:
                            part_of_xr(0, "xr", r + 2, "high")
                        if u == U - 2:
                            part_of_xr(1, "rest", r + 2, "mid")
                        if u == U - 1:
                            act.wait_ge(s["seeded"], r + 1)
                            publish_parts()
                        act.wait_ge(s["preg_a"], now)
                        nc.scalar.activation(first.g, first.pre_g, ACT.Tanh, scale=scale)
                        act.wait_ge(s["pre_a"], now)
                        nc.scalar.activation(first.i_f, first.pre_if, ACT.Sigmoid, scale=scale).then_inc(s["if_a"], 1)
                        act.wait_ge(s["preo_a"], now)
                        nc.scalar.activation(first.o, first.pre_o[:], ACT.Sigmoid, scale=scale)
                        act.wait_ge(s["c_a"], now)
                        nc.scalar.activation(first.tanh_c, first.c, ACT.Tanh).then_inc(s["tc_a"], 1)
                        act.wait_ge(s["pre_b"], now)
                        nc.scalar.activation(second.g, second.pre_g, ACT.Tanh, scale=scale)
                        nc.scalar.activation(second.i_f, second.pre_if, ACT.Sigmoid, scale=scale).then_inc(s["if_b"], 1)
                        act.wait_ge(s["preo_b"], now)
                        nc.scalar.activation(second.o, second.pre_o[:], ACT.Sigmoid, scale=scale)
                        act.wait_ge(s["c_b"], now)
                        nc.scalar.activation(second.tanh_c, second.c, ACT.Tanh).then_inc(s["tc_b"], 1)

            act.wait_ge(s["usual"], 1)
            usual = act.value_load(usual_i[0:1, 0:1], min_val=0, max_val=1)
            with act.If(usual != 0):
                steps(1.0 / (W_TOP * H_SCALE))
            with act.Else():
                steps(inv[:])

        @block.vector
        def _(dve):
            nc.vector.memset(first.c, 0.0)
            nc.vector.memset(second.c, 0.0).then_inc(s["zero"], 1)
            for k in range(NC):
                wh_arrived(dve, [k])
                nc.vector.tensor_reduce(amaxk[:, k:k + 1], stage[:, k, :], AX.X, ALU.max, apply_absolute_value=True).then_inc(s["amaxk"], 1)
            dve.wait_ge(s["amaxk"], NC)
            nc.vector.tensor_reduce(amax[:], amaxk[:], AX.X, ALU.max, apply_absolute_value=True).then_inc(s["amax"], 1)
            dve.wait_ge(s["amaxall"], 1)
            nc.vector.tensor_scalar(e2[:].bitcast(I32), amaxall[:].bitcast(I32), 0x7F800000, None, ALU.bitwise_and).then_inc(s["exponent"], 1)
            dve.wait_ge(s["exponent"], 1)
            nc.vector.tensor_scalar(e2[:], e2[:], 2.0 ** -80, 2.0 ** 80, ALU.max, ALU.min).then_inc(s["exponent"], 1)
            dve.wait_ge(s["exponent"], 2)
            nc.vector.tensor_scalar(low[:], e2[:], USUAL[0], None, ALU.is_ge).then_inc(s["exponent"], 1)
            dve.wait_ge(s["exponent"], 3)
            nc.vector.scalar_tensor_tensor(low[:], e2[:], USUAL[1], low[:], ALU.is_le, ALU.mult).then_inc(s["exponent"], 1)
            nc.vector.tensor_scalar(one_less[:], e2[:], -1.0, 1.0, ALU.mult, ALU.add).then_inc(s["exponent"], 1)
            dve.wait_ge(s["exponent"], 5)
            nc.vector.tensor_copy(usual_i[:], low[:]).then_inc(s["usual"], 1)
            nc.vector.scalar_tensor_tensor(e2[:], one_less[:], low[:], e2[:], ALU.mult, ALU.add).then_inc(s["exponent"], 1)
            dve.wait_ge(s["exponent"], 6)
            nc.vector.reciprocal(rcp[:], e2[:]).then_inc(s["rcp"], 1)
            dve.wait_ge(s["rcp"], 1)
            nc.vector.tensor_scalar(sc[:], rcp[:], W_TOP, None, ALU.mult).then_inc(s["sc"], 1)
            nc.vector.tensor_scalar(inv[:], e2[:], 1.0 / (W_TOP * H_SCALE), None, ALU.mult).then_inc(s["rcp"], 1)
            dve.wait_ge(s["sc"], 1)
            nc.vector.tensor_scalar(outv[:], sc[:], H_SCALE, None, ALU.mult).then_inc(s["rcp"], 1)
            dve.wait_ge(s["rcp"], 3)
            dve.wait_ge(s["sel1"], 1)
            nc.vector.tensor_scalar(SEL[:].rearrange("p u j m -> p (u j m)"), SEL[:].rearrange("p u j m -> p (u j m)"), outv[:], None,
                                    ALU.mult).then_inc(s["sel"], 1)

            def rest_of_xr(n):
                dve.wait_ge(s["high"], n)
                nc.vector.tensor_tensor(XR[:], XR[:], XM[:, 0], ALU.subtract).then_inc(s["rest"], 1)

            def last_part_of_xr(n):
                dve.wait_ge(s["mid"], n)
                nc.vector.tensor_tensor(XP[:, 2], XR[:], XM[:, 1], ALU.subtract).then_inc(s["low"], 1)

            for k in range(NC):
                dve.wait_ge(s["hi"], k + 1)
                for j in range(NJ):
                    view = lambda part: w16[:, part, k, j, :].rearrange("p (gc i) -> p gc i", i=Q)
                    nc.vector.scalar_tensor_tensor(view(1), tile_cols(stage, k, j, 0, NG), sc[:], view(0),
                                                   ALU.mult, ALU.subtract).then_inc(s["lo"], 1)
                if k == 0:
                    dve.wait_ge(s["bias"], 16 * len(RUNS) * NF * NJ)
                    dve.wait_ge(s["xw"], 1)
                    nc.vector.tensor_tensor(XR[:], PX[:], bias[:], ALU.add).then_inc(s["xr"], 1)
                if k == 1:
                    rest_of_xr(1)
                if k == 2:
                    last_part_of_xr(1)
            dve.wait_ge(s["zero"], 1)
            nc.vector.memset(H[:, 0, 0:NF], 0.0).then_inc(s["h_a"], 1)
            nc.vector.memset(H[:, 0, NF:], 0.0).then_inc(s["h_b"], 1)

            def transposed(bank, start, lo, hi):
                return nc.vector.transpose(wide(GT[:, lo:hi, :]), bank[:, (lo - start) * Q:(hi - start) * Q])

            def both_parts(dst, lo, hi):
                return nc.vector.tensor_tensor(dst, GT[:, lo:hi, 0:B], GT[:, lo:hi, B:2 * B], ALU.add)

            def multiply(group, x, now):
                dve.wait_ge(s["if_" + x], now)
                nc.vector.tensor_tensor(group.igfc[:], group.i_f, group.g_and_c, ALU.mult).then_inc(s["ig_" + x], 1)

            def new_c(group, x, now):
                dve.wait_ge(s["ig_" + x], now)
                nc.vector.tensor_tensor(group.c, group.igfc[:, 0:NF * B], group.igfc[:, NF * B:], ALU.add).then_inc(s["c_" + x], 1)

            def high_h(group, x, u, now):
                dve.wait_ge(s["tc_" + x], now)
                nc.vector.tensor_tensor(HH[:, u, group.cols], group.o, group.tanh_c, ALU.mult)
                nc.vector.scalar_tensor_tensor(H[:, (u + 1) % 2, group.chunks, 0:B], by_unit(group.o), H_SCALE, by_unit(group.tanh_c),
                                               ALU.mult, ALU.mult).then_inc(s["hi_" + x], 1)

            def low_h(group, x, u, now):
                dve.wait_ge(s["hi_" + x], now)
                nxt = H[:, (u + 1) % 2, group.chunks, :]
                nc.vector.scalar_tensor_tensor(nxt[:, :, B:2 * B], by_unit(HH[:, u, group.cols]), H_SCALE, nxt[:, :, 0:B],
                                               ALU.mult, ALU.subtract).then_inc(s["h_" + x], 1)

            with dve.Fori(0, rounds) as r:
                for u in range(U):
                    now = dve.snap(r * U + (u + 1))
                    if u == U - 3:
                        dve.wait_ge(s["xw"], r + 2)
                        nc.vector.tensor_tensor(XR[:], PX[:], bias[:], ALU.add).then_inc(s["xr"], 1)
                    if u == U - 2:
                        rest_of_xr(r + 2)
                    if u == U - 1:
                        dve.wait_ge(s["seeded"], r + 1)
                        last_part_of_xr(r + 2)
                    dve.wait_ge(s["gates_a"], now)
                    transposed(PA, 0, 0, NF).then_inc(s["trg_a"], 1)
                    transposed(PA, 0, NF, 3 * NF).then_inc(s["trif_a"], 1)
                    dve.wait_ge(s["trg_a"], now)
                    both_parts(by_unit(first.pre_g), 0, NF).then_inc(s["preg_a"], 1)
                    dve.wait_ge(s["trif_a"], now)
                    both_parts(by_unit(first.pre_if), NF, 3 * NF).then_inc(s["pre_a"], 1)
                    transposed(PA, 0, 3 * NF, GA).then_inc(s["tr_a"], 1)
                    dve.wait_ge(s["tr_a"], now)
                    both_parts(by_unit(first.pre_o[:]), 3 * NF, GA).then_inc(s["preo_a"], 1)
                    multiply(first, "a", now)
                    dve.wait_ge(s["gates_b"], now)
                    transposed(PB, GA, GA, GA + NF)
                    new_c(first, "a", now)
                    if u == 0:
                        dve.wait_ge(s["xadd"], r + 1)
                    transposed(PB, GA, GA + NF, GA + 3 * NF).then_inc(s["trif_b"], 1)
                    transposed(PB, GA, GA + 3 * NF, NG).then_inc(s["tr_b"], 1)
                    dve.wait_ge(s["trif_b"], now)
                    both_parts(by_unit(PREB[:, 0:3 * NF * B]), GA, GA + 3 * NF).then_inc(s["pre_b"], 1)
                    high_h(first, "a", u, now)
                    dve.wait_ge(s["tr_b"], now)
                    both_parts(by_unit(second.pre_o[:]), GA + 3 * NF, NG).then_inc(s["preo_b"], 1)
                    low_h(first, "a", u, now)
                    multiply(second, "b", now)
                    new_c(second, "b", now)
                    high_h(second, "b", u, now)
                    low_h(second, "b", u, now)
            dve.wait_ge(s["xadd"], rounds + 1)


def gated_scan(nc, m, biases2, pad, weights, wx, wh, ahead):
    with ExitStack() as ctx:
        s = Sems(nc, ctx, "g_", "next tw cw z f i gs rg fn inm ni ln one lc ex0 ex1 sn hid sum out small")
        sbt = lambda n, shape, dt=F32: ctx.enter_context(nc.sbuf_tensor("g_" + n, shape, dt))
        banks = [ctx.enter_context(nc.psum_tensor(f"g_z{i}", [P, 512], F32)) for i in range(8)]
        TBB = P * B
        natural = m.natural_weights()
        wt = m.scratch[:, 0:3 * NC * D].rearrange("p (w k h) -> p w k h", w=3, k=NC)
        F = sbt("F", [P, 2, TBB])
        I = sbt("I", [P, 2, TBB])
        GS = sbt("GS", [P, TBB])
        LC = sbt("LC", [P, 2, T + 1])
        ni_buf = [m.scratch[:, 3 * NC * D + i * XCOLS:3 * NC * D + (i + 1) * XCOLS] for i in range(2)]
        items = [(c, n) for c in range(NC) for n in range(TB)]
        block = ctx.enter_context(nc.Block())
        row = lambda a, b: a.rearrange("p (t b) -> p b t", b=B)[:, b, :]
        lr = lambda c: m.xb[:, c, 0:XCOLS]

        def blocks_and_scans(on_block, on_first, on_second):
            for c, n in items:
                if c < NC:
                    on_block(c, n, c * TB + n)
                if 0 < c < NC:
                    (on_second if n % 2 else on_first)(c - 1, n // 2, (c - 1) * B + n // 2)
            c = NC - 1
            on_first(c, 0, c * B)
            for b in range(B):
                if b + 1 < B:
                    on_first(c, b + 1, c * B + b + 1)
                on_second(c, b, c * B + b)

        @block.sync
        def _(sp):
            with nc.allow_non_contiguous_dma(reason="small vectors, features to partitions"):
                for dst, src in biases2:
                    sp.dma_start(dst, src).then_inc(s["small"], 16)
            sp.wait_ge(s["small"], 16 * len(biases2))
            sp.wait_ge(s["z"], 3 * NC * TB)
            sp.wait_ge(s["out"], (NC - 1) * B)
            load_weight(weights[0], wx, sp, s["next"])
            load_weight(weights[1], wh, sp, s["next"], range(ahead))
            sp.wait_ge(s["next"], 16 * len(RUNS) * (NC + ahead))

        @block.gpsimd
        def _(pool):
            nc.gpsimd.memset(pad, 0.0)
            for q in range(NC * B):
                c, b = divmod(q, B)
                pool.wait_ge(s["sum"], q + 1)
                nc.gpsimd.tensor_tensor(row(lr(c), b), row(lr(c), b), row(m.xa[:, c, 0:XCOLS], b), ALU.add).then_inc(s["out"], 1)

        @block.tensor
        def _(pe):
            for n in range(3 * NC):
                w, k = divmod(n, NC)
                if n >= 8:
                    pe.wait_ge(s["cw"], n - 7)
                for h in range(NC):
                    last = nc.tensor.transpose(banks[n % 8][:, h * P:(h + 1) * P], natural[:, w * NC + h, k * P:(k + 1) * P], m.ident[:])
                last.then_inc(s["tw"], 1)
            pe.wait_ge(s["cw"], 3 * NC)
            for n in range(NC * TB):
                c, blk = divmod(n, TB)
                if n >= 2:
                    pe.wait_ge(s["f"], n - 1)
                    pe.wait_ge(s["i"], n - 1)
                    pe.wait_ge(s["ni"], n - 1)
                for w in range(3):
                    for k in range(NC):
                        last = nc.tensor.matmul(banks[w * 2 + n % 2][:], wt[:, w, k, c * P:(c + 1) * P],
                                                m.xa[:, k, blk * TBB:(blk + 1) * TBB], start=(k == 0), stop=(k == NC - 1))
                    last.then_inc(s["z"], 1)

        @block.scalar
        def _(act):
            act.wait_ge(s["small"], 16 * len(biases2))

            def gates(c, blk, n):
                act.wait_ge(s["z"], 3 * n + 1)
                if n >= 2:
                    act.wait_ge(s["ni"], n - 1)
                nc.scalar.activation(F[:, n % 2], banks[n % 2][:], ACT.Sigmoid, bias=m.bias2[:, 0, c:c + 1]).then_inc(s["f"], 1)
                act.wait_ge(s["z"], 3 * n + 2)
                nc.scalar.activation(I[:, n % 2], banks[2 + n % 2][:], ACT.Sigmoid, bias=m.bias2[:, 1, c:c + 1]).then_inc(s["i"], 1)
                act.wait_ge(s["fn"], n + 1)
                nc.scalar.activation(lr(c)[:, blk * TBB:(blk + 1) * TBB], F[:, n % 2], ACT.Ln, bias=m.eps[:]).then_inc(s["ln"], 1)

            def exponentials(c, b, q):
                act.wait_ge(s["lc"], q + 1)
                lc = LC[:, q % 2]
                nc.scalar.activation(row(lr(c), b), lc[:, 0:T], ACT.Exp, scale=-1.0, bias=lc[:, T:T + 1]).then_inc(s["ex0"], 1)
                act.wait_ge(s["ex0"], q + 1)
                nc.scalar.activation(lc[:, 1:T + 1], lc[:, 1:T + 1], ACT.Exp).then_inc(s["ex1"], 1)

            blocks_and_scans(gates, exponentials, lambda c, b, q: None)

        @block.vector
        def _(dve):
            nc.vector.memset(LC[:, :, 0:1], 0.0).then_inc(s["one"], 1)
            for n in range(3 * NC):
                w, k = divmod(n, NC)
                dve.wait_ge(s["tw"], n + 1)
                nc.vector.tensor_copy(wt[:, w, k, :], banks[n % 8][:]).then_inc(s["cw"], 1)
            dve.wait_ge(s["one"], 1)
            dve.wait_ge(s["small"], 16 * len(biases2))
            running = m.one[:].broadcast_to([P, T])

            def ratios(c, blk, n):
                f, i = F[:, n % 2], I[:, n % 2]
                dve.wait_ge(s["f"], n + 1)
                dve.wait_ge(s["i"], n + 1)
                nc.vector.scalar_tensor_tensor(GS[:], f, 1e-8, i, ALU.add, ALU.add).then_inc(s["gs"], 1)
                dve.wait_ge(s["gs"], n + 1)
                nc.vector.reciprocal(GS[:], GS[:]).then_inc(s["rg"], 1)
                dve.wait_ge(s["rg"], n + 1)
                nc.vector.tensor_tensor(f, f, GS[:], ALU.mult).then_inc(s["fn"], 1)
                nc.vector.tensor_tensor(i, i, GS[:], ALU.mult).then_inc(s["inm"], 1)
                dve.wait_ge(s["inm"], n + 1)
                dve.wait_ge(s["z"], 3 * n + 3)
                if blk == 0 and c >= 2:
                    dve.wait_ge(s["hid"], (c - 1) * B)
                nc.vector.scalar_tensor_tensor(ni_buf[c % 2][:, blk * TBB:(blk + 1) * TBB], banks[4 + n % 2][:],
                                               m.bias2[:, 2, c:c + 1], i, ALU.add, ALU.mult).then_inc(s["ni"], 1)

            def log_scan(c, b, q):
                dve.wait_ge(s["ln"], (c + 1) * TB)
                if q >= 2:
                    dve.wait_ge(s["sum"], q - 1)
                nc.vector.tensor_tensor_scan(LC[:, q % 2, 1:T + 1], running, row(lr(c), b), 0.0, ALU.mult, ALU.add).then_inc(s["lc"], 1)

            def hidden_scan(c, b, q):
                ni = row(ni_buf[c % 2], b)
                dve.wait_ge(s["ni"], (c + 1) * TB)
                dve.wait_ge(s["ex0"], q + 1)
                nc.vector.tensor_tensor(ni, ni, row(lr(c), b), ALU.mult).then_inc(s["sn"], 1)
                dve.wait_ge(s["sn"], q + 1)
                nc.vector.tensor_tensor_scan(row(lr(c), b), running, ni, 0.0, ALU.mult, ALU.add).then_inc(s["hid"], 1)
                dve.wait_ge(s["hid"], q + 1)
                dve.wait_ge(s["ex1"], q + 1)
                nc.vector.scalar_tensor_tensor(row(lr(c), b), LC[:, q % 2, 1:T + 1], m.cond[:, c, b:b + 1], row(lr(c), b),
                                               ALU.mult, ALU.add).then_inc(s["sum"], 1)

            blocks_and_scans(ratios, log_scan, hidden_scan)


def store(nc, m, out):
    with ExitStack() as ctx:
        s = Sems(nc, ctx, "s_", "tp cpv cps out")
        tp = [ctx.enter_context(nc.psum_tensor(f"s_tp{i}", [P, 512], F32)) for i in range(8)]
        xo = m.xa_all[:, 0:B * TB * D].rearrange("p (n d) -> p n d", d=D)
        block = ctx.enter_context(nc.Block())

        @block.tensor
        def _(pe):
            for n in range(B * TB):
                b, tb = divmod(n, TB)
                if n >= 8:
                    pe.wait_ge(s["cpv"] if n % 2 == 0 else s["cps"], (n - 8) // 2 + 1)
                for c in range(NC):
                    src = m.xb[:, c, 0:XCOLS].rearrange("p (t b) -> p b t", b=B)[:, b, tb * P:(tb + 1) * P]
                    last = nc.tensor.transpose(tp[n % 8][:, c * P:(c + 1) * P], src, m.ident[:])
                last.then_inc(s["tp"], 1)

        @block.vector
        def _(dve):
            for n in range(0, B * TB, 2):
                dve.wait_ge(s["tp"], n + 1)
                nc.vector.tensor_copy(xo[:, n, :], tp[n % 8][:]).then_inc(s["cpv"], 1)

        @block.scalar
        def _(act):
            for n in range(1, B * TB, 2):
                act.wait_ge(s["tp"], n + 1)
                nc.scalar.activation(xo[:, n, :], tp[n % 8][:], ACT.Copy).then_inc(s["cps"], 1)

        @block.sync
        def _(sp):
            for n in range(0, B * TB, 2):
                b, tb = divmod(n, TB)
                sp.wait_ge(s["cpv"], n // 2 + 1)
                sp.wait_ge(s["cps"], n // 2 + 1)
                sp.dma_start(out[b, tb * P:(tb + 2) * P, :].rearrange("(n p) d -> p n d", p=P), xo[:, n:n + 2, :]).then_inc(s["out"], 16)
            sp.wait_ge(s["out"], 16 * (B * TB // 2))


class Memory:

    def __init__(self, nc, ctx):
        sbt = lambda n, shape: ctx.enter_context(nc.sbuf_tensor(n, shape, F32))
        self.xa_all = sbt("xa", [P, NC * XCOLS + XTAIL])
        self.xb_all = sbt("xb", [P, NC * XCOLS + XTAIL])
        self.scratch = sbt("scratch", [P, 14 * T])
        self.xa = self.xa_all[:, 0:NC * XCOLS].rearrange("p (c n) -> p c n", c=NC)
        self.xb = self.xb_all[:, 0:NC * XCOLS].rearrange("p (c n) -> p c n", c=NC)
        self.ident = sbt("ident", [P, P])
        self.cond = sbt("cond", [P, NC, B])
        self.bias2 = sbt("bias2", [P, 3, NC])
        self.eps = sbt("eps", [P, 1])
        self.one = sbt("one", [P, 1])
        self.small = sbt("small", [P, 7 * B * NC])

    def natural_weights(self):
        return self.scratch[:, NC * G4:NC * G4 + 3 * NC * D].rearrange("p (n d) -> p n d", d=D)

    def lstm_weights(self, region):
        half = NC * G4
        fp32 = [region[:, i * half:(i + 1) * half].rearrange("p (k n) -> p k n", k=NC) for i in range(2)]
        parts = self.scratch[:, 0:half].bitcast(F16).rearrange("p (s k j n) -> p s k j n", s=2, k=NC, j=NJ)
        return fp32 + [parts]


def program(nc, x, cond, wx1, wh1, b1, wf, bf, wi, bi, wh, bh, wx3, wh3, b3, out):
    with ExitStack() as ctx:
        m = Memory(nc, ctx)

        units = lambda b: b.rearrange("(c p) -> p c", p=P)
        weights1, weights3 = m.lstm_weights(m.xb_all), m.lstm_weights(m.xa_all)
        ahead = ((NC - 1) * XCOLS - NC * G4) // G4
        natural = m.natural_weights()
        load_and_sparsify(nc, m, x, cond, [(weights1[0], wx1), (weights1[1], wh1)])
        lstm(nc, m, "p_", m.xa_all, weights1, wh1, b1, NC,
             also_load=[(natural[:, w * NC:(w + 1) * NC, :], a.rearrange("(h p) d -> p h d", p=P)) for w, a in enumerate((wf, wi, wh))])
        gated_scan(nc, m, [(m.bias2[:, w, :], units(b)) for w, b in enumerate((bf, bi, bh))], m.xb_all[:, NC * XCOLS:],
                   weights3, wx3, wh3, ahead)
        lstm(nc, m, "q_", m.xb_all, weights3, wh3, b3, ahead)
        store(nc, m, out)


_INS = ['x', 'cond_1024', 'L1_cond_Wx', 'L1_cond_Wh', 'L1_cond_b', 'L2_cond_W_f', 'L2_cond_b_f', 'L2_cond_W_i',
        'L2_cond_b_i', 'L2_cond_W_h', 'L2_cond_b_h', 'L3_cond_Wx', 'L3_cond_Wh', 'L3_cond_b']


def kernel(**inputs):
    import numpy as _np
    import concourse.bacc as _bacc
    from concourse import mybir as _mybir
    from concourse.bass_utils import run_bass_kernel_spmd as _run

    nc = _bacc.Bacc("TRN2", target_bir_lowering=False, num_devices=1)
    arrays, args = {}, []
    for name in _INS:
        a = _np.ascontiguousarray(inputs[name])
        arrays[f"in_{name}_dram"] = a
        args.append(nc.dram_tensor(f"in_{name}_dram", a.shape, _mybir.dt.from_np(a.dtype), kind="ExternalInput").ap())
    args.append(nc.dram_tensor("out_0_dram", (B, T, D), _mybir.dt.float32, kind="ExternalOutput").ap())
    program(nc, *args)
    r = _run(nc, [arrays], core_ids=[0])
    return r.results[0]["out_0_dram"]
```
